# Optimizing a Trainium2 kernel written in Bass

```python
import numpy as np
import jax
import jax.numpy as jnp

def _softmax(x, axis=-1):
    return jax.nn.softmax(x, axis=axis)
def _gelu(x):
    return jax.nn.gelu(x, approximate=True)
def _silu(x):
    return jax.nn.silu(x)
def _sigmoid(x):
    return jax.nn.sigmoid(x)
def _layernorm(x, axis=-1, eps=1e-5):
    m = jnp.mean(x, axis=axis, keepdims=True)
    v = jnp.var(x, axis=axis, keepdims=True)
    return (x - m) / jnp.sqrt(v + eps)
def _scatter_add(tgt, idx, src, axis=0):
    return tgt.at[idx].add(src)
def _segment_sum(src, seg, n):
    return jax.ops.segment_sum(src, seg, n)

kernel_name = 'mk_adj_resnorm_d2_adj_512_050c91'

def setup_inputs(seed: int = 0):
    np.random.seed(seed)
    _w = jnp.asarray
    def _rec_inputs():
        import jax
        import jax.numpy as jnp
        _gk = jax.random.key(seed)
        x = -0.0002928 + 1 * jax.random.normal(jax.random.fold_in(_gk, 1), (3327, 512), jnp.float32)
        _a = jax.random.bernoulli(jax.random.fold_in(_gk, 2), 0.00961827, (3327, 3327))
        _af = _a.astype(jnp.float32)
        adj = _af
        return x, adj
    x, adj = _rec_inputs()
    def _L0_gnn_setup():
        import jax, jax.numpy as jnp
        import numpy as np
        N = 8192
        D = 512
        L = 2
        NEG_SLOPE = 0.01

        def _gat_layer(x, W, adj):
            proj = x @ W
            Wh, Ws = jnp.split(proj, 2, axis=-1)
            scores = Wh @ Ws.T
            a = jax.nn.softmax(scores, axis=-1) * adj
            out = a @ Wh
            out = out + x
            return jax.nn.leaky_relu(out, NEG_SLOPE)
        key = jax.random.key(seed)
        k1, k2, k3 = jax.random.split(key, 3)
        inputs = jax.random.normal(k1, (N, D), dtype=jnp.float32)
        adj = jax.random.randint(k2, (N, N), 0, 2).astype(jnp.float32)
        W_stack = jax.random.normal(k3, (L, D, 2 * D), dtype=jnp.float32) * (1.0 / np.sqrt(D))
        return {'inputs': inputs, 'adj': adj, 'W_stack': W_stack}
    _L0_gnn_all = _L0_gnn_setup()
    _L0_gnn_in = {k: v for k, v in _L0_gnn_all.items() if k in ('W_stack', )}
    del _L0_gnn_all

    def _L1_gnn_setup():
        import jax, jax.numpy as jnp
        import numpy as np

        def _bin_sign(v):
            return jnp.sign(v)

        def _bin_sign_z(v):
            return jnp.maximum(jnp.sign(v), 0.0)
        key = jax.random.key(seed)
        k1, k2, k3 = jax.random.split(key, 3)
        N, D_IN, D_OUT = (8192, 512, 512)
        x = jax.random.normal(k1, (N, D_IN), dtype=jnp.float32)
        support = jax.random.uniform(k2, (N, N), dtype=jnp.float32)
        weight = jax.random.normal(k3, (D_OUT, D_IN), dtype=jnp.float32)
        return {'x': x, 'support': support, 'weight': weight}
    _L1_gnn_all = _L1_gnn_setup()
    _L1_gnn_in = {k: v for k, v in _L1_gnn_all.items() if k in ('weight', )}
    del _L1_gnn_all

    return {
        "x": x,
        "adj": adj,
        "L0_gnn_W_stack": _L0_gnn_in["W_stack"],
        "L1_gnn_weight": _L1_gnn_in["weight"],
    }

def reference(x, adj, L0_gnn_W_stack, L1_gnn_weight):
    import jax
    import jax.numpy as jnp
    def _L0_gnn_ref(inputs, adj, W_stack):
        import jax, jax.numpy as jnp
        import numpy as np
        N = 8192
        D = 512
        L = 2
        NEG_SLOPE = 0.01

        def _gat_layer(x, W, adj):
            proj = x @ W
            Wh, Ws = jnp.split(proj, 2, axis=-1)
            scores = Wh @ Ws.T
            a = jax.nn.softmax(scores, axis=-1) * adj
            out = a @ Wh
            out = out + x
            return jax.nn.leaky_relu(out, NEG_SLOPE)
        x = inputs
        for l in range(W_stack.shape[0]):
            x = _gat_layer(x, W_stack[l], adj)
        return x

    def _L1_gnn_ref(x, support, weight):
        import jax, jax.numpy as jnp
        import numpy as np

        def _bin_sign(v):
            return jnp.sign(v)

        def _bin_sign_z(v):
            return jnp.maximum(jnp.sign(v), 0.0)
        bw = _bin_sign(weight)
        ba = _bin_sign_z(x)
        xw = ba @ bw.T
        out = support @ xw
        return jax.nn.relu(out)

    x = _layernorm(x + _L0_gnn_ref(x, adj, L0_gnn_W_stack), axis=-1)
    x = _layernorm(x + _L1_gnn_ref(x, adj, L1_gnn_weight), axis=-1)
    return x


_drawn_inputs = setup_inputs


def setup_inputs(seed=0):
    import zlib

    import numpy as np

    out = dict(_drawn_inputs(seed))
    spreads = {}
    factors = {}
    for name, (base, spread) in spreads.items():
        noise = np.random.default_rng([zlib.crc32(name.encode()), seed]).standard_normal(out[name].shape)
        drawn = base * np.exp(spread * noise) if base else spread * noise
        out[name] = jnp.asarray(drawn.astype(out[name].dtype))
    for name, factor in factors.items():
        out[name] = (out[name] * factor).astype(out[name].dtype)
    return out
```

```python
from contextlib import ExitStack

import concourse.bass as bass
from concourse import mybir
from concourse.alu_op_type import AluOpType as ALU

ACT = mybir.ActivationFunctionType
F32 = mybir.dt.float32
F32R = mybir.dt.float32r
F16 = mybir.dt.float16
U32 = mybir.dt.uint32
AX_X = mybir.AxisListType.X
REDUCE_MAX = bass.bass_isa.ReduceOp.max

P = 128
HI, LO = 0, 1
BANK = 512
SLOPE = 0.01
EPS = 1e-5
PROB_SCALE = 1024.0
TOP = 2.0 ** 14
LOWEST = -3.0e38
LEAST_BOUND = 1e-30
EXPONENT_BITS = 0x7F800000


def ceil_div(a, b):
    return -(-a // b)


def row_tiles(engine, tiles):
    for t in (0, 1):
        yield t, t
    with engine.Fori(1, tiles // 2 - 1) as pair:
        for b in (0, 1):
            yield pair * 2 + b, b
    for t in (tiles - 2, tiles - 1):
        yield t, t % 2


def fixed(t):
    return isinstance(t, int)


def from_tile(t, first):
    return not fixed(t) or t >= first


def before_end(t, ahead, tiles):
    return not fixed(t) or t + ahead < tiles


def landed(t, b, transfers=1):
    return (t - b) * (8 * transfers) + 16 * transfers


class Chain:

    def __init__(self, engine, sem, per_tile=0):
        self.engine, self.sem, self.per_tile = engine, sem, per_tile
        self.base, self.done = 0, 0

    def tile(self, t):
        self.base, self.done = t * self.per_tile, 0

    def link(self, instruction):
        self.done += 1
        instruction.then_inc(self.sem, 1)
        self.engine.wait_ge(self.sem, self.base + self.done)


def build(nc, N, x, adj, adj_t, w_stack, weight, identity, out):
    NP, D = x.shape
    T = NP // P
    DC = D // P
    LAYERS = w_stack.shape[0]
    assert T % 2 == 0 and D == BANK

    with ExitStack() as whole:
        def sem(name):
            return whole.enter_context(nc.semaphore(name))

        def keep(name, shape, dt):
            return whole.enter_context(nc.sbuf_tensor(name, shape, dt))

        kept = {
            "ident": keep("ident", [P, P], F32),
            "ident16": keep("ident16", [P, P], F16),
            "ones": keep("ones", [P, P], F32),
            "scales": keep("scales", [P, 8], F32),
            "row_norm": keep("row_norm", [P, 1], F32),
            "var_eps": keep("var_eps", [P, T], F32),
        }
        x_mid = nc.dram_tensor("x_mid", [NP, D], F32, kind="Internal").ap()
        centred = nc.dram_tensor("centred", [NP, D], F32, kind="Internal").ap()

        constants(nc, sem, identity, kept)
        layer_in = x
        for layer in range(LAYERS):
            last = layer == LAYERS - 1
            layer_out = centred if last else x_mid
            with ExitStack() as s:
                values = s.enter_context(nc.sbuf_tensor(f"values{layer}", [P, 2, T, D], F16))
                keys_t = s.enter_context(nc.sbuf_tensor(f"keys_t{layer}", [P, 2, DC, NP], F16))
                project(nc, sem, layer, layer_in, w_stack, kept, values, keys_t, T, DC, D)
                attend(nc, sem, layer, layer_in, x, adj, layer_out, kept, values, keys_t,
                       N, NP, T, DC, D, last)
            layer_in = x_mid
        with ExitStack() as s:
            products = s.enter_context(nc.sbuf_tensor("products", [P, T, D], F32R))
            binary_products(nc, sem, centred, weight, kept, products, T, DC, D)
            binary_aggregate(nc, sem, centred, adj_t, out, kept, products, NP, T, D)


def constants(nc, sem, identity, kept):
    loaded, made = sem("identity_loaded"), sem("constants_made")
    with nc.Block() as block:
        @block.sync
        def _(sp):
            sp.dma_start(kept["ident"][:], identity).then_inc(loaded, 16)

        @block.vector
        def _(dve):
            dve.memset(kept["ones"][:], 1.0).then_inc(made, 1)
            dve.memset(kept["row_norm"][:], 0.0).then_inc(made, 1)
            dve.wait_ge(loaded, 16)
            dve.tensor_copy(kept["ident16"][:], kept["ident"][:]).then_inc(made, 1)
            dve.wait_ge(made, 3)


SCALE, KEY_SCALE_INV2, NEG_INV2, OUT_SCALE = 0, 1, 2, 3


def project(nc, sem, layer, x_in, w_stack, kept, values, keys_t, T, DC, D):
    ident, ident16, ones, scales = kept["ident"], kept["ident16"], kept["ones"], kept["scales"]
    row_norm = kept["row_norm"]
    W2 = w_stack.shape[2]
    PAIRS = T // 2

    def named(name):
        return sem(f"{name}_p{layer}")

    w_loaded, w_split, squared = (named(n) for n in ("w_loaded", "w_split", "squared"))
    x_loaded = [named(f"x_loaded{b}") for b in (0, 1)]
    norms_loaded = [named(f"norms_loaded{b}") for b in (0, 1)]
    norms_done, norm_ready = named("norms_done"), named("norm_ready")
    columns_done, all_norm, bound_ready, root_ready, scale_ready = (
        named(n) for n in ("columns_done", "all_norm", "bound_ready", "root_ready", "scale_ready"))
    x_turned, x_hi, x_lo = named("x_turned"), named("x_hi"), named("x_lo")
    values_done, keys_done, values_hi, keys_hi = (
        named(n) for n in ("values_done", "keys_done", "values_hi", "keys_hi"))
    values_lo, keys_lo, keys_turned, keys_stored, own = (
        named(n) for n in ("values_lo", "keys_lo", "keys_turned", "keys_stored", "dve_chain"))

    with ExitStack() as s:
        def sb(name, shape, dt):
            return s.enter_context(nc.sbuf_tensor(f"{name}_p{layer}", shape, dt))

        def ps(name, shape, dt):
            return s.enter_context(nc.psum_tensor(f"{name}_p{layer}", shape, dt))

        w_raw = sb("w_raw", [P, DC, W2], F32)
        w_sq = sb("w_sq", [P, DC, W2], F32)
        w = sb("w", [P, 2, DC, W2], F32R)
        rows2 = sb("rows2", [P, 2, 2 * D], F32)
        norms = sb("norms", [P, PAIRS], F32)
        small = sb("small", [P, 8], F32)
        exponent = sb("exponent", [P, 1], U32)
        x_rows = sb("x_rows", [P, 2, D], F32)
        x_t = sb("x_t", [P, 2, 2, D], F32R)
        keys = sb("keys", [P, 2, 2, D], F16)
        turned_x = ps("turned_x", [P, 2, BANK], F32)
        p_values = ps("p_values", [P, 2, BANK], F32)
        p_keys = ps("p_keys", [P, 2, BANK], F32)
        turned_k = ps("turned_k", [P, 2, 2, DC, P], F16)
        column_norms = p_values

        with nc.Block() as block:
            @block.sync
            def _(sp):
                sp.dma_start(w_raw[:], w_stack[layer].rearrange("(c p) n -> p c n", p=P)).then_inc(w_loaded, 16)
                if layer == 0:
                    pairs = x_in.rearrange("(j p two) d -> j p (two d)", p=P, two=2)
                    for j in range(PAIRS):
                        if j >= 2:
                            sp.wait_ge(norms_done, j - 1)
                        sp.dma_start(rows2[:, j % 2], pairs[j]).then_inc(norms_loaded[j % 2], 16)
                for t, b in row_tiles(sp, T):
                    if from_tile(t, 2):
                        sp.wait_ge(x_turned, t - 1)
                    sp.dma_start(x_rows[:, b], x_in[bass.ds(t * P, P), :]).then_inc(x_loaded[b], 16)

            @block.gpsimd
            def _(pool):
                pool.wait_ge(norm_ready, 1)
                pool.partition_all_reduce(small[:, 1:2], row_norm[:], P, REDUCE_MAX).then_inc(all_norm, 1)

            @block.scalar
            def _(act):
                act.wait_ge(w_loaded, 16)
                act.activation(w_sq[:], w_raw[:], ACT.Square).then_inc(squared, 1)
                if layer == 0:
                    for j in range(PAIRS):
                        act.wait_ge(norms_loaded[j % 2], 16 * (j // 2 + 1))
                        act.activation(rows2[:, j % 2], rows2[:, j % 2], ACT.Square,
                                       accum_out=norms[:, j:j + 1]).then_inc(norms_done, 1)
                act.wait_ge(bound_ready, 1)
                act.activation(small[:, 3:4], small[:, 2:3], ACT.Sqrt).then_inc(root_ready, 1)

                def halve_x(t, b):
                    act.wait_ge(x_turned, t + 1)
                    if from_tile(t, 2):
                        act.wait_ge(keys_done, t - 1)
                    act.activation(x_t[:, b, HI], turned_x[:, b], ACT.Copy).then_inc(x_hi, 1)

                halve_x(0, 0)
                act.wait_ge(scale_ready, 1)
                for t, b in row_tiles(act, T):
                    if before_end(t, 1, T):
                        halve_x(t + 1, 1 - b)
                    act.wait_ge(values_done, t + 1)
                    act.wait_ge(scale_ready, 1)
                    act.activation(values[:, HI, bass.ds(t, 1), :], p_values[:, b:b + 1], ACT.Copy,
                                   scale=scales[:, SCALE:SCALE + 1]).then_inc(values_hi, 1)
                    act.wait_ge(keys_done, t + 1)
                    if from_tile(t, 2):
                        act.wait_ge(keys_turned, t - 1)
                    act.activation(keys[:, b, HI], p_keys[:, b], ACT.Copy,
                                   scale=scales[:, SCALE:SCALE + 1]).then_inc(keys_hi, 1)

            @block.vector
            def _(dve):
                chain = Chain(dve, own)
                dve.wait_ge(w_loaded, 16)
                dve.tensor_copy(w[:, HI], w_raw[:]).then_inc(w_split, 1)
                dve.wait_ge(w_split, 1)
                dve.tensor_tensor(w[:, LO], w_raw[:], w[:, HI].bitcast(F32), ALU.subtract).then_inc(w_split, 1)
                if layer == 0:
                    dve.wait_ge(norms_done, PAIRS)
                    chain.link(dve.reduce_max(row_norm[:], norms[:], AX_X))
                dve.tensor_copy(small[:, 4:5], row_norm[:]).then_inc(norm_ready, 1)
                dve.wait_ge(columns_done, 1)
                chain.link(dve.reduce_max(small[:, 0:1], column_norms[:].rearrange("p a b -> p (a b)"), AX_X))
                dve.wait_ge(all_norm, 1)
                chain.link(dve.tensor_tensor(small[:, 5:6], small[:, 0:1], small[:, 1:2], ALU.mult))
                dve.tensor_scalar(small[:, 2:3], small[:, 5:6], LEAST_BOUND, None, ALU.max).then_inc(bound_ready, 1)
                chain.link(dve.memset(exponent[:], EXPONENT_BITS))
                dve.wait_ge(root_ready, 1)
                chain.link(dve.reciprocal(small[:, 6:7], small[:, 3:4]))
                chain.link(dve.tensor_scalar(small[:, 7:8], small[:, 6:7], TOP, None, ALU.mult))
                chain.link(dve.tensor_tensor(scales[:, SCALE:SCALE + 1].bitcast(U32),
                                             small[:, 7:8].bitcast(U32), exponent[:], ALU.bitwise_and))
                chain.link(dve.reciprocal(small[:, 6:7], scales[:, SCALE:SCALE + 1]))
                chain.link(dve.tensor_tensor(scales[:, KEY_SCALE_INV2:KEY_SCALE_INV2 + 1],
                                             small[:, 6:7], small[:, 6:7], ALU.mult))
                chain.link(dve.tensor_scalar(scales[:, NEG_INV2:NEG_INV2 + 1],
                                             scales[:, KEY_SCALE_INV2:KEY_SCALE_INV2 + 1], -1.0, None, ALU.mult))
                dve.tensor_scalar(scales[:, OUT_SCALE:OUT_SCALE + 1], small[:, 6:7],
                                  1.0 / PROB_SCALE, None, ALU.mult).then_inc(scale_ready, 1)
                scale = scales[:, SCALE:SCALE + 1]

                def halve_x(t, b):
                    dve.wait_ge(x_hi, t + 1)
                    dve.tensor_tensor(x_t[:, b, LO], turned_x[:, b], x_t[:, b, HI].bitcast(F32),
                                      ALU.subtract).then_inc(x_lo, 1)

                def store_keys(t, b):
                    dve.wait_ge(keys_turned, t + 1)
                    dve.tensor_scalar(keys_t[:, :, :, bass.ds(t * P, P)], turned_k[:, b], 1.0, None,
                                      ALU.mult).then_inc(keys_stored, 1)

                halve_x(0, 0)
                for t, b in row_tiles(dve, T):
                    if before_end(t, 1, T):
                        halve_x(t + 1, 1 - b)
                    if from_tile(t, 1):
                        store_keys(t - 1, 1 - b)
                    dve.wait_ge(values_hi, t + 1)
                    dve.scalar_tensor_tensor(out=values[:, LO, bass.ds(t, 1), :], in0=p_values[:, b:b + 1],
                                             scalar=scale, in1=values[:, HI, bass.ds(t, 1), :],
                                             op0=ALU.mult, op1=ALU.subtract).then_inc(values_lo, 1)
                    dve.wait_ge(keys_hi, t + 1)
                    dve.scalar_tensor_tensor(out=keys[:, b, LO], in0=p_keys[:, b], scalar=scale,
                                             in1=keys[:, b, HI], op0=ALU.mult,
                                             op1=ALU.subtract).then_inc(keys_lo, 1)
                store_keys(T - 1, (T - 1) % 2)

            @block.tensor
            def _(pe):
                def turn_x(t, b):
                    pe.wait_ge(x_loaded[b], landed(t, b))
                    if from_tile(t, 2):
                        pe.wait_ge(x_lo, t - 1)
                    for c in range(DC):
                        last = pe.transpose(turned_x[:, b, c * P:(c + 1) * P],
                                            x_rows[:, b, c * P:(c + 1) * P], ident[:])
                    last.then_inc(x_turned, 1)

                def product(bank, b, columns):
                    parts = [(HI, HI), (HI, LO), (LO, HI)]
                    for c in range(DC):
                        for n, (xh, wh) in enumerate(parts):
                            last = pe.matmul(bank, x_t[:, b, xh, c * P:(c + 1) * P], w[:, wh, c, columns],
                                             start=(c == 0 and n == 0), stop=(c == DC - 1 and n == 2))
                    return last

                def turn_keys(t, b):
                    pe.wait_ge(keys_lo, t + 1)
                    if from_tile(t, 2):
                        pe.wait_ge(keys_stored, t - 1)
                    for half in (HI, LO):
                        for c in range(DC):
                            last = pe.transpose(turned_k[:, b, half, c, :],
                                                keys[:, b, half, c * P:(c + 1) * P], ident16[:])
                    last.then_inc(keys_turned, 1)

                turn_x(0, 0)
                pe.wait_ge(squared, 1)
                for half in range(W2 // BANK):
                    for c in range(DC):
                        last = pe.matmul(column_norms[:, half], ones[:],
                                         w_sq[:, c, half * BANK:(half + 1) * BANK],
                                         start=(c == 0), stop=(c == DC - 1))
                last.then_inc(columns_done, 1)
                pe.wait_ge(w_split, 2)
                pe.wait_ge(bound_ready, 1)
                for t, b in row_tiles(pe, T):
                    if before_end(t, 1, T):
                        turn_x(t + 1, 1 - b)
                    pe.wait_ge(x_lo, t + 1)
                    if from_tile(t, 2):
                        pe.wait_ge(values_lo, t - 1)
                    product(p_values[:, b], b, slice(0, D)).then_inc(values_done, 1)
                    if from_tile(t, 1):
                        turn_keys(t - 1, 1 - b)
                    if from_tile(t, 2):
                        pe.wait_ge(keys_lo, t - 1)
                    product(p_keys[:, b], b, slice(D, 2 * D)).then_inc(keys_done, 1)
                turn_keys(T - 1, (T - 1) % 2)


def attend(nc, sem, layer, x_in, x_first, adj, rows_out, kept, values, keys_t, N, NP, T, DC, D, last_layer):
    ident, ident16, ones, scales = kept["ident"], kept["ident16"], kept["ones"], kept["scales"]
    row_norm, var_eps = kept["row_norm"], kept["var_eps"]
    KC = ceil_div(NP, BANK)
    widths = [min(BANK, NP - k * BANK) for k in range(KC)]
    valid = [min(BANK, N - k * BANK) for k in range(KC)]
    PARTS = 4
    PART = NP // PARTS
    GROUP = BANK // P
    G = ceil_div(T, GROUP)
    members = [range(g * GROUP, min(T, (g + 1) * GROUP)) for g in range(G)]
    LINKS = 9 if last_layer else 6

    def named(name):
        return sem(f"{name}_a{layer}")

    adj_loaded, x_loaded, stored = (
        [named(f"{n}{b}") for b in (0, 1)] for n in ("adj_loaded", "x_loaded", "stored"))
    q_staged, q_turned, q_ready = (named(n) for n in ("q_staged", "q_turned", "q_ready"))
    scores_done, scores_read, shift_ready = (named(n) for n in ("scores_done", "scores_read", "shift_ready"))
    exp_done, masked, pad_zeroed = (named(n) for n in ("exp_done", "masked", "pad_zeroed"))
    probs_turned, probs_hi, probs_split, mixed = (
        named(n) for n in ("probs_turned", "probs_hi", "probs_split", "mixed"))
    rows_done, own, peak_own = (named(n) for n in ("rows_done", "dve_chain", "peak_chain"))

    with ExitStack() as s:
        def sb(name, shape, dt):
            return s.enter_context(nc.sbuf_tensor(f"{name}_a{layer}", shape, dt))

        def ps(name, shape, dt):
            return s.enter_context(nc.psum_tensor(f"{name}_a{layer}", shape, dt))

        row = sb("row", [P, 2, NP], F32)
        adj_row = sb("adj_row", [P, 2, NP], F32)
        probs = sb("probs", [P, G, 2, GROUP * P], F16)
        q_rows = sb("q_rows", [P, 2, D], F16)
        q_t = sb("q_t", [P, 2, 2, DC, P], F16)
        peaks = sb("peaks", [P, 2, KC + 1], F32)
        shift = sb("shift", [P, 2], F32)
        sums = sb("sums", [P, 2, PARTS], F32)
        small = sb("small", [P, 16], F32)
        stats = sb("stats", [P, 8], F32)
        waited = sb("waited", [P, 1], F32)
        x_rows = sb("x_rows", [P, 2, D], F32)
        x0_rows = sb("x0_rows", [P, 2, D], F32) if last_layer else None
        work = sb("work", [P, 2, D], F32)
        y_rows = sb("y_rows", [P, 2, D], F32)
        p_scores = ps("p_scores", [P, 2, BANK], F32)
        p_probs = ps("p_probs", [P, 2, BANK], F32)
        p_out = ps("p_out", [P, 2, BANK], F32)
        p_q = ps("p_q", [P, 2, DC, P], F16)
        X_LOADS = 2 if last_layer else 1

        with nc.Block() as block:
            @block.sync
            def _(sp):
                def store(t, b):
                    sp.dma_start(rows_out[bass.ds(t * P, P), :], y_rows[:, b]).then_inc(stored[b], 16)

                for t, b in row_tiles(sp, T):
                    if from_tile(t, 2):
                        sp.wait_ge(masked, PARTS * (t - 1))
                    sp.dma_start(adj_row[:, b], adj[bass.ds(t * P, P), :]).then_inc(adj_loaded[b], 16)
                    if from_tile(t, 2):
                        sp.wait_ge(rows_done, t - 1)
                        store(t - 2, b)
                    sp.dma_start(x_rows[:, b], x_in[bass.ds(t * P, P), :]).then_inc(x_loaded[b], 16)
                    if last_layer:
                        sp.dma_start(x0_rows[:, b], x_first[bass.ds(t * P, P), :]).then_inc(x_loaded[b], 16)
                for t in (T - 2, T - 1):
                    sp.wait_ge(rows_done, t + 1)
                    store(t, t % 2)
                for b in (0, 1):
                    sp.wait_ge(stored[b], 16 * (T // 2))

            @block.tensor
            def _(pe):
                def turn_q(t):
                    pe.wait_ge(q_staged, t + 1)
                    if from_tile(t, 1):
                        pe.wait_ge(q_ready, t)
                    for half in (HI, LO):
                        for c in range(DC):
                            last = pe.transpose(p_q[:, half, c, :], q_rows[:, half, c * P:(c + 1) * P], ident16[:])
                    last.then_inc(q_turned, 1)

                def scores(t, b):
                    pe.wait_ge(q_ready, t + 1)
                    for k in range(KC):
                        bank = (b * KC + k) % 2
                        if from_tile(t, 1) or k >= 2:
                            pe.wait_ge(scores_read, t * KC + k - 1)
                        n = 0
                        for c in range(DC):
                            for qh, kh in ((HI, HI), (HI, LO), (LO, HI)):
                                last = pe.matmul(p_scores[:, bank, 0:widths[k]], q_t[:, b, qh, c, :],
                                                 keys_t[:, kh, c, k * BANK:k * BANK + widths[k]],
                                                 start=(n == 0), stop=(n == 3 * DC - 1))
                                n += 1
                        last.then_inc(scores_done, 1)

                def turn_probs(t, b, g):
                    if from_tile(t, 1) or g >= 2:
                        pe.wait_ge(probs_split, t * G + g - 1)
                    for j, k in enumerate(members[g]):
                        last = pe.transpose(p_probs[:, (b * G + g) % 2, j * P:(j + 1) * P],
                                            row[:, b, k * P:(k + 1) * P], ident[:])
                    last.then_inc(probs_turned, 1)

                def mix(t, b, g):
                    pe.wait_ge(probs_split, t * G + g + 1)
                    for j, k in enumerate(members[g]):
                        for n, (ph, vh) in enumerate(((HI, HI), (HI, LO), (LO, HI))):
                            last = pe.matmul(p_out[:, b], probs[:, g, ph, j * P:(j + 1) * P], values[:, vh, k, :],
                                             start=(k == 0 and n == 0), stop=(k == T - 1 and n == 2))
                    last.then_inc(mixed, 1)

                turn_q(0)
                turn_q(1)
                scores(0, 0)
                for t, b in row_tiles(pe, T):
                    if before_end(t, 1, T):
                        scores(t + 1, 1 - b)
                    pe.wait_ge(masked, PARTS * (t + 1))
                    turn_probs(t, b, 0)
                    turn_probs(t, b, 1)
                    if before_end(t, 2, T):
                        turn_q(t + 2)
                    if from_tile(t, 2):
                        pe.wait_ge(rows_done, t - 1)
                    for g in range(G):
                        mix(t, b, g)
                        if g + 2 < G:
                            turn_probs(t, b, g + 2)

            @block.scalar
            def _(act):
                def exp_part(t, b, part):
                    if part == 0:
                        if from_tile(t, 2):
                            act.wait_ge(rows_done, t - 1)
                        act.wait_ge(shift_ready, t + 1)
                    piece = row[:, b, part * PART:min(N, (part + 1) * PART)]
                    act.activation(piece, piece, ACT.Exp, bias=shift[:, b:b + 1],
                                   scale=scales[:, KEY_SCALE_INV2:KEY_SCALE_INV2 + 1],
                                   accum_out=sums[:, b, part:part + 1]).then_inc(exp_done, 1)

                for part in range(PARTS):
                    exp_part(0, 0, part)
                for t, b in row_tiles(act, T):
                    for g in range(G):
                        act.wait_ge(probs_turned, t * G + g + 1)
                        used = len(members[g]) * P
                        act.activation(probs[:, g, HI, 0:used], p_probs[:, (b * G + g) % 2, 0:used],
                                       ACT.Copy, scale=PROB_SCALE).then_inc(probs_hi, 1)
                        if 1 <= g <= PARTS and before_end(t, 1, T):
                            exp_part(t + 1, 1 - b, g - 1)

            @block.gpsimd
            def _(pool):
                for t, b in row_tiles(pool, T):
                    pool.wait_ge(adj_loaded[b], landed(t, b))
                    pool.wait_ge(pad_zeroed, 2)
                    for part in range(PARTS):
                        pool.wait_ge(exp_done, t * PARTS + part + 1)
                        piece = slice(part * PART, (part + 1) * PART)
                        pool.tensor_tensor(row[:, b, piece], row[:, b, piece], adj_row[:, b, piece],
                                           ALU.mult).then_inc(masked, 1)

            @block.vector
            def _(dve):
                peak_chain, chain = Chain(dve, peak_own, 1), Chain(dve, own, LINKS)

                def stage_q(t):
                    if from_tile(t, 1):
                        dve.wait_ge(q_turned, t)
                    dve.tensor_scalar(q_rows[:].rearrange("p (h o) d -> p h o d", o=1),
                                      values[:, :, bass.ds(t, 1), :], 1.0, None, ALU.mult).then_inc(q_staged, 1)

                def copy_q(t, b):
                    dve.wait_ge(q_turned, t + 1)
                    if from_tile(t, 2):
                        dve.wait_ge(scores_done, (t - 1) * KC)
                    dve.tensor_copy(q_t[:, b], p_q[:]).then_inc(q_ready, 1)

                def read_scores(t, b, k):
                    if k == 0 and from_tile(t, 2):
                        dve.wait_ge(probs_turned, (t - 1) * G)
                    dve.wait_ge(scores_done, t * KC + k + 1)
                    dve.wait_ge(pad_zeroed, 2)
                    w = valid[k]
                    dve.tensor_scalar(row[:, b, k * BANK:k * BANK + w], p_scores[:, (b * KC + k) % 2, 0:w],
                                      1.0, LOWEST, ALU.mult, ALU.max,
                                      accum_out=peaks[:, b, k:k + 1]).then_inc(scores_read, 1)

                def make_shift(t, b):
                    peak_chain.tile(t)
                    dve.wait_ge(scores_read, (t + 1) * KC)
                    peak_chain.link(dve.reduce_max(peaks[:, b, KC:KC + 1], peaks[:, b, 0:KC], AX_X))
                    dve.tensor_tensor(shift[:, b:b + 1], peaks[:, b, KC:KC + 1],
                                      scales[:, NEG_INV2:NEG_INV2 + 1], ALU.mult).then_inc(shift_ready, 1)

                def split_probs(t, b, g):
                    dve.wait_ge(probs_hi, t * G + g + 1)
                    used = len(members[g]) * P
                    dve.scalar_tensor_tensor(out=probs[:, g, LO, 0:used], in0=p_probs[:, (b * G + g) % 2, 0:used],
                                             scalar=PROB_SCALE, in1=probs[:, g, HI, 0:used],
                                             op0=ALU.mult, op1=ALU.subtract).then_inc(probs_split, 1)

                def finish(t, b):
                    chain.tile(t)
                    r = small[:, 8 * b:8 * b + 8]
                    dve.wait_ge(mixed, (t + 1) * G)
                    chain.link(dve.reduce_sum(r[:, 0:1], sums[:, b], AX_X))
                    chain.link(dve.reciprocal(r[:, 1:2], r[:, 0:1]))
                    chain.link(dve.tensor_tensor(r[:, 2:3], r[:, 1:2], scales[:, OUT_SCALE:OUT_SCALE + 1], ALU.mult))
                    dve.wait_ge(x_loaded[b], landed(t, b, X_LOADS))
                    chain.link(dve.scalar_tensor_tensor(out=work[:, b], in0=p_out[:, b], scalar=r[:, 2:3],
                                                        in1=x_rows[:, b], op0=ALU.mult, op1=ALU.add))
                    if from_tile(t, 2):
                        dve.wait_ge(stored[b], landed(t - 2, b))
                    if not last_layer:
                        chain.link(dve.scalar_tensor_tensor(out=y_rows[:, b], in0=work[:, b], scalar=SLOPE,
                                                            in1=work[:, b], op0=ALU.mult, op1=ALU.max))
                        chain.link(dve.tensor_tensor_reduce(work[:, b], y_rows[:, b], y_rows[:, b], 1.0, 0.0,
                                                            ALU.mult, ALU.add, r[:, 3:4]))
                        dve.tensor_tensor(row_norm[:], row_norm[:], r[:, 3:4], ALU.max).then_inc(rows_done, 1)
                    else:
                        chain.link(dve.scalar_tensor_tensor(out=y_rows[:, b], in0=work[:, b], scalar=SLOPE,
                                                            in1=work[:, b], op0=ALU.mult, op1=ALU.max))
                        chain.link(dve.tensor_tensor(work[:, b], y_rows[:, b], x0_rows[:, b], ALU.add))
                        chain.link(dve.bn_stats(stats[:, 0:6], work[:, b]))
                        dve.memset(waited[:], 0.0)
                        chain.link(dve.bn_aggr(stats[:, 6:8], stats[:, 0:6]))
                        chain.link(dve.tensor_scalar(var_eps[:, bass.ds(t, 1)], stats[:, 7:8], EPS, None, ALU.add))
                        dve.tensor_scalar(y_rows[:, b], work[:, b], stats[:, 6:7], None,
                                          ALU.subtract).then_inc(rows_done, 1)
                    assert chain.done == LINKS

                for b in (0, 1):
                    dve.memset(row[:, b, N:NP], 0.0).then_inc(pad_zeroed, 1)
                stage_q(0)
                copy_q(0, 0)
                stage_q(1)
                copy_q(1, 1)
                for k in range(KC):
                    read_scores(0, 0, k)
                make_shift(0, 0)
                for t, b in row_tiles(dve, T):
                    if before_end(t, 1, T):
                        for k in range(KC):
                            read_scores(t + 1, 1 - b, k)
                        make_shift(t + 1, 1 - b)
                    if before_end(t, 2, T):
                        stage_q(t + 2)
                    for g in range(G):
                        split_probs(t, b, g)
                        if g == 1 and before_end(t, 2, T):
                            copy_q(t + 2, b)
                    finish(t, b)




def binary_products(nc, sem, centred, weight, kept, products, T, DC, D):
    ident, ident16, var_eps = kept["ident"], kept["ident16"], kept["var_eps"]
    rows_loaded = [sem(f"rows_loaded{b}_c") for b in (0, 1)]
    names = ("weight_loaded", "weight_turned", "signs_made", "above", "rows_turned",
             "rows_copied", "products_done", "products_kept", "roots", "rstd_made")
    (weight_loaded, weight_turned, signs_made, above, rows_turned,
     rows_copied, products_done, products_kept, roots, rstd_made) = (sem(f"{n}_c") for n in names)

    with ExitStack() as s:
        def sb(name, shape, dt):
            return s.enter_context(nc.sbuf_tensor(f"{name}_c", shape, dt))

        def ps(name, shape, dt):
            return s.enter_context(nc.psum_tensor(f"{name}_c", shape, dt))

        w_rows = sb("w_rows", [P, DC, D], F32)
        positive = sb("positive", [P, DC, D], F16)
        negative = sb("negative", [P, DC, D], F16)
        signs_t = sb("signs_t", [P, DC, D], F16)
        rows = sb("rows", [P, 2, D], F32)
        bits = sb("bits", [P, 2, D], F16)
        bits_t = sb("bits_t", [P, 2, DC * P], F16)
        root = sb("root", [P, T], F32)
        p_w = ps("p_w", [P, DC, BANK], F32)
        p_bits = ps("p_bits", [P, 2, 2 * BANK], F16)
        p_out = ps("p_out", [P, 2, BANK], F32)

        with nc.Block() as block:
            @block.sync
            def _(sp):
                sp.dma_start(w_rows[:], weight.rearrange("(r p) n -> p r n", p=P)).then_inc(weight_loaded, 16)
                for t, b in row_tiles(sp, T):
                    if from_tile(t, 2):
                        sp.wait_ge(above, t - 1)
                    sp.dma_start(rows[:, b], centred[bass.ds(t * P, P), :]).then_inc(rows_loaded[b], 16)

            @block.tensor
            def _(pe):
                pe.wait_ge(weight_loaded, 16)
                for c in range(DC):
                    for r in range(DC):
                        last = pe.transpose(p_w[:, c, r * P:(r + 1) * P], w_rows[:, r, c * P:(c + 1) * P], ident[:])
                last.then_inc(weight_turned, 1)

                def turn(t, b):
                    pe.wait_ge(above, t + 1)
                    if from_tile(t, 2):
                        pe.wait_ge(rows_copied, t - 1)
                    for c in range(DC):
                        last = pe.transpose(p_bits[:, b, c * P:(c + 1) * P], bits[:, b, c * P:(c + 1) * P], ident16[:])
                    last.then_inc(rows_turned, 1)

                turn(0, 0)
                pe.wait_ge(signs_made, 3)
                for t, b in row_tiles(pe, T):
                    if before_end(t, 1, T):
                        turn(t + 1, 1 - b)
                    pe.wait_ge(rows_copied, t + 1)
                    if from_tile(t, 2):
                        pe.wait_ge(products_kept, t - 1)
                    for c in range(DC):
                        last = pe.matmul(p_out[:, b], bits_t[:, b, c * P:(c + 1) * P], signs_t[:, c],
                                         start=(c == 0), stop=(c == DC - 1))
                    last.then_inc(products_done, 1)

            @block.scalar
            def _(act):
                act.activation(root[:], var_eps[:], ACT.Sqrt).then_inc(roots, 1)

                def copy_bits(t, b):
                    act.wait_ge(rows_turned, t + 1)
                    if from_tile(t, 2):
                        act.wait_ge(products_done, t - 1)
                    act.activation(bits_t[:, b], p_bits[:, b, 0:DC * P], ACT.Copy).then_inc(rows_copied, 1)

                copy_bits(0, 0)
                for t, b in row_tiles(act, T):
                    if before_end(t, 1, T):
                        copy_bits(t + 1, 1 - b)
                    act.wait_ge(products_done, t + 1)
                    act.wait_ge(roots, 1)
                    act.activation(products[:, bass.ds(t, 1), :], p_out[:, b:b + 1], ACT.Copy).then_inc(products_kept, 1)

            @block.vector
            def _(dve):
                dve.wait_ge(roots, 1)
                dve.reciprocal(var_eps[:], root[:]).then_inc(rstd_made, 1)
                dve.wait_ge(weight_turned, 1)
                dve.tensor_scalar(positive[:], p_w[:], 0.0, None, ALU.is_gt).then_inc(signs_made, 1)
                dve.tensor_scalar(negative[:], p_w[:], 0.0, None, ALU.is_lt).then_inc(signs_made, 1)
                dve.wait_ge(signs_made, 2)
                dve.tensor_tensor(signs_t[:], positive[:], negative[:], ALU.subtract).then_inc(signs_made, 1)
                for t, b in row_tiles(dve, T):
                    dve.wait_ge(rows_loaded[b], landed(t, b))
                    if from_tile(t, 2):
                        dve.wait_ge(rows_turned, t - 1)
                    dve.tensor_scalar(bits[:, b], rows[:, b], 0.0, None, ALU.is_gt).then_inc(above, 1)


def binary_aggregate(nc, sem, centred, adj_t, out, kept, products, NP, T, D):
    rstd = kept["var_eps"]
    LINKS = 5
    adj_loaded, rows_loaded, stored = (
        [sem(f"{n}{b}_d") for b in (0, 1)] for n in ("adj_loaded", "rows_loaded", "stored"))
    names = ("adj_hi_made", "adj_lo_made", "sums_done", "var_made", "std_made", "rows_done", "dve_chain")
    (adj_hi_made, adj_lo_made, sums_done, var_made, std_made, rows_done, own) = (sem(f"{n}_d") for n in names)

    with ExitStack() as s:
        def sb(name, shape, dt):
            return s.enter_context(nc.sbuf_tensor(f"{name}_d", shape, dt))

        adj_raw = sb("adj_raw", [P, 2, T * P], F32)
        adj_hi = sb("adj_hi", [P, 2, T * P], F32R)
        adj_lo = sb("adj_lo", [P, 2, T * P], F32R)
        rows = sb("rows", [P, 2, D], F32)
        work = sb("work", [P, 2, D], F32)
        y_rows = sb("y_rows", [P, 2, D], F32)
        stats = sb("stats", [P, 2, 8], F32)
        std = sb("std", [P, 2, 4], F32)
        waited = sb("waited", [P, 1], F32)
        p_sum = s.enter_context(nc.psum_tensor("p_sum_d", [P, 2, BANK], F32))

        with nc.Block() as block:
            @block.sync
            def _(sp):
                def store(t, b):
                    sp.dma_start(out[bass.ds(t * P, P), :], y_rows[:, b]).then_inc(stored[b], 16)

                for t, b in row_tiles(sp, T):
                    if from_tile(t, 2):
                        sp.wait_ge(adj_lo_made, t - 1)
                    sp.dma_start(adj_raw[:, b], adj_t[bass.ds(t * P, P), :]).then_inc(adj_loaded[b], 16)
                    if from_tile(t, 2):
                        sp.wait_ge(rows_done, t - 1)
                        store(t - 2, b)
                    sp.dma_start(rows[:, b], centred[bass.ds(t * P, P), :]).then_inc(rows_loaded[b], 16)
                for t in (T - 2, T - 1):
                    sp.wait_ge(rows_done, t + 1)
                    store(t, t % 2)
                for b in (0, 1):
                    sp.wait_ge(stored[b], 16 * (T // 2))

            @block.scalar
            def _(act):
                def copy_hi(t, b):
                    act.wait_ge(adj_loaded[b], landed(t, b))
                    if from_tile(t, 2):
                        act.wait_ge(sums_done, t - 1)
                    act.activation(adj_hi[:, b], adj_raw[:, b], ACT.Copy).then_inc(adj_hi_made, 1)

                copy_hi(0, 0)
                for t, b in row_tiles(act, T):
                    if before_end(t, 1, T):
                        copy_hi(t + 1, 1 - b)
                    act.wait_ge(var_made, t + 1)
                    act.activation(std[:, b, 1:2], std[:, b, 0:1], ACT.Sqrt).then_inc(std_made, 1)

            @block.tensor
            def _(pe):
                for t, b in row_tiles(pe, T):
                    pe.wait_ge(adj_lo_made, t + 1)
                    if from_tile(t, 2):
                        pe.wait_ge(rows_done, t - 1)
                    for k in range(T):
                        for half in (adj_hi, adj_lo):
                            last = pe.matmul(p_sum[:, b], half[:, b, k * P:(k + 1) * P], products[:, k, :],
                                             start=(k == 0 and half is adj_hi),
                                             stop=(k == T - 1 and half is adj_lo))
                    last.then_inc(sums_done, 1)

            @block.vector
            def _(dve):
                chain = Chain(dve, own, LINKS)

                def make_lo(t, b):
                    dve.wait_ge(adj_hi_made, t + 1)
                    dve.tensor_tensor(adj_lo[:, b], adj_raw[:, b], adj_hi[:, b].bitcast(F32),
                                      ALU.subtract).then_inc(adj_lo_made, 1)

                make_lo(0, 0)
                for t, b in row_tiles(dve, T):
                    if before_end(t, 1, T):
                        make_lo(t + 1, 1 - b)
                    chain.tile(t)
                    dve.wait_ge(rows_loaded[b], landed(t, b))
                    chain.link(dve.tensor_scalar(work[:, b], rows[:, b], rstd[:, bass.ds(t, 1)], None, ALU.mult))
                    dve.wait_ge(sums_done, t + 1)
                    chain.link(dve.scalar_tensor_tensor(out=work[:, b], in0=p_sum[:, b], scalar=0.0,
                                                        in1=work[:, b], op0=ALU.max, op1=ALU.add))
                    chain.link(dve.bn_stats(stats[:, b, 0:6], work[:, b]))
                    dve.memset(waited[:], 0.0)
                    chain.link(dve.bn_aggr(stats[:, b, 6:8], stats[:, b, 0:6]))
                    dve.tensor_scalar(std[:, b, 0:1], stats[:, b, 7:8], EPS, None, ALU.add).then_inc(var_made, 1)
                    dve.wait_ge(std_made, t + 1)
                    chain.link(dve.reciprocal(std[:, b, 2:3], std[:, b, 1:2]))
                    if from_tile(t, 2):
                        dve.wait_ge(stored[b], landed(t - 2, b))
                    dve.tensor_scalar(y_rows[:, b], work[:, b], stats[:, b, 6:7], std[:, b, 2:3],
                                      ALU.subtract, ALU.mult).then_inc(rows_done, 1)
                    assert chain.done == LINKS


def kernel(x, adj, L0_gnn_W_stack, L1_gnn_weight):
    import numpy as np
    import concourse.bacc as bacc
    from concourse.bass_utils import run_bass_kernel_spmd

    x, adj = np.asarray(x), np.asarray(adj)
    n, d = x.shape
    padded = ceil_div(n, P) * P
    tiles = padded // P
    x_rows = np.zeros((padded, d), x.dtype)
    x_rows[:n] = x
    adj_rows = np.zeros((padded, padded), adj.dtype)
    adj_rows[:n, :n] = adj
    adj_blocks = np.ascontiguousarray(adj_rows.reshape(tiles, P, tiles, P).transpose(0, 3, 2, 1))
    arrays = {
        "x_rows": x_rows,
        "adj_rows": adj_rows,
        "adj_blocks": adj_blocks.reshape(padded, padded),
        "w_stack": np.ascontiguousarray(L0_gnn_W_stack),
        "weight": np.ascontiguousarray(L1_gnn_weight),
        "identity": np.eye(P, dtype=np.float32),
    }
    nc = bacc.Bacc("TRN2", target_bir_lowering=False, num_devices=1)
    aps = [nc.dram_tensor(name, a.shape, mybir.dt.from_np(a.dtype), kind="ExternalInput").ap()
           for name, a in arrays.items()]
    result = nc.dram_tensor("result", (padded, d), F32, kind="ExternalOutput").ap()
    build(nc, n, *aps, result)
    got = run_bass_kernel_spmd(nc, [arrays], core_ids=[0])
    return got.results[0]["result"][:n]
```

```python
from contextlib import ExitStack

import concourse.bass as bass
from concourse import mybir
from concourse.alu_op_type import AluOpType as ALU

ACT = mybir.ActivationFunctionType
F32 = mybir.dt.float32
F32R = mybir.dt.float32r
F16 = mybir.dt.float16
U32 = mybir.dt.uint32
AX_X = mybir.AxisListType.X
REDUCE_MAX = bass.bass_isa.ReduceOp.max

P = 128
HI, LO = 0, 1
BANK = 512
SLOPE = 0.01
EPS = 1e-5
PARTS = 4
PROB_SCALE = 1024.0
TOP = 2.0 ** 14
LOWEST = -3.0e38
LEAST_BOUND = 1e-30
LOW_BITS = 0xFFF
EXPONENT_BITS = 0x7F800000


def ceil_div(a, b):
    return -(-a // b)


def row_tiles(engine, tiles):
    for t in (0, 1):
        yield t, t
    with engine.Fori(1, tiles // 2 - 1) as pair:
        for b in (0, 1):
            yield pair * 2 + b, b
    for t in (tiles - 2, tiles - 1):
        yield t, t % 2


def fixed(t):
    return isinstance(t, int)


def from_tile(t, first):
    return not fixed(t) or t >= first


def before_end(t, ahead, tiles):
    return not fixed(t) or t + ahead < tiles


def landed(t, b, transfers=1):
    return (t - b) * (8 * transfers) + 16 * transfers


class Chain:

    def __init__(self, engine, sem, per_tile=0):
        self.engine, self.sem, self.per_tile = engine, sem, per_tile
        self.base, self.done = 0, 0

    def tile(self, t):
        self.base, self.done = t * self.per_tile, 0

    def link(self, instruction):
        self.done += 1
        instruction.then_inc(self.sem, 1)
        self.engine.wait_ge(self.sem, self.base + self.done)


def build(nc, N, x, adj, adj_t, w_stack, weight, identity, out):
    NP, D = x.shape
    T = NP // P
    DC = D // P
    LAYERS = w_stack.shape[0]
    assert T % 2 == 0 and D == BANK

    with ExitStack() as whole:
        def sem(name):
            return whole.enter_context(nc.semaphore(name))

        def keep(name, shape, dt):
            return whole.enter_context(nc.sbuf_tensor(name, shape, dt))

        kept = {
            "ident": keep("ident", [P, P], F32),
            "ident16": keep("ident16", [P, P], F16),
            "ones": keep("ones", [P, P], F32),
            "scales": keep("scales", [P, 8], F32),
            "row_norm": keep("row_norm", [P, 1], F32),
            "var_eps": keep("var_eps", [P, T], F32),
            "adj_low": keep("adj_low", [P, T * PARTS], F32),
        }
        x_mid = nc.dram_tensor("x_mid", [NP, D], F32, kind="Internal").ap()
        centred = nc.dram_tensor("centred", [NP, D], F32, kind="Internal").ap()

        constants(nc, sem, identity, kept)
        layer_in = x
        w_raw = keep("w_raw", [P, DC, w_stack.shape[2]], F32)
        w_loaded = sem("w_loaded")
        for layer in range(LAYERS):
            last = layer == LAYERS - 1
            layer_out = centred if last else x_mid
            with ExitStack() as s:
                values = s.enter_context(nc.sbuf_tensor(f"values{layer}", [P, 2, T, D], F16))
                keys_t = s.enter_context(nc.sbuf_tensor(f"keys_t{layer}", [P, 2, DC, NP], F16))
                project(nc, sem, layer, layer_in, w_stack, w_raw, w_loaded, kept, values, keys_t, T, DC, D)
                attend(nc, sem, layer, layer_in, x, adj, layer_out, kept, values, keys_t,
                       w_stack, w_raw, w_loaded, N, NP, T, DC, D, last)
            layer_in = x_mid
        binary_layer(nc, sem, centred, weight, adj_t, out, kept, T, DC, D)


def constants(nc, sem, identity, kept):
    loaded, made = sem("identity_loaded"), sem("constants_made")
    with nc.Block() as block:
        @block.sync
        def _(sp):
            sp.dma_start(kept["ident"][:], identity).then_inc(loaded, 16)

        @block.vector
        def _(dve):
            dve.memset(kept["ones"][:], 1.0).then_inc(made, 1)
            dve.memset(kept["row_norm"][:], 0.0).then_inc(made, 1)
            dve.wait_ge(loaded, 16)
            dve.tensor_copy(kept["ident16"][:], kept["ident"][:]).then_inc(made, 1)
            dve.wait_ge(made, 3)


SCALE, KEY_SCALE_INV2, NEG_INV2, OUT_SCALE = 0, 1, 2, 3


def load_weights(sp, w_stack, layer, w_raw, w_loaded):
    sp.dma_start(w_raw[:], w_stack[layer].rearrange("(c p) n -> p c n", p=P)).then_inc(w_loaded, 16)


def project(nc, sem, layer, x_in, w_stack, w_raw, w_loaded, kept, values, keys_t, T, DC, D):
    ident, ident16, ones, scales = kept["ident"], kept["ident16"], kept["ones"], kept["scales"]
    row_norm = kept["row_norm"]
    W2 = w_stack.shape[2]
    PAIRS = T // 2

    def named(name):
        return sem(f"{name}_p{layer}")

    w_split, squared = named("w_split"), named("squared")
    x_loaded = [named(f"x_loaded{b}") for b in (0, 1)]
    norms_loaded = [named(f"norms_loaded{b}") for b in (0, 1)]
    norms_done, norm_ready, ones_made = named("norms_done"), named("norm_ready"), named("ones_made")
    columns_done, all_norm, bound_ready, root_ready, scale_ready = (
        named(n) for n in ("columns_done", "all_norm", "bound_ready", "root_ready", "scale_ready"))
    x_turned, x_hi, x_lo = named("x_turned"), named("x_hi"), named("x_lo")
    values_done, keys_done, values_hi, keys_hi = (
        named(n) for n in ("values_done", "keys_done", "values_hi", "keys_hi"))
    values_lo, keys_lo, keys_turned, keys_stored, own = (
        named(n) for n in ("values_lo", "keys_lo", "keys_turned", "keys_stored", "dve_chain"))

    with ExitStack() as s:
        def sb(name, shape, dt):
            return s.enter_context(nc.sbuf_tensor(f"{name}_p{layer}", shape, dt))

        def ps(name, shape, dt):
            return s.enter_context(nc.psum_tensor(f"{name}_p{layer}", shape, dt))

        w_sq = sb("w_sq", [P, DC, W2], F32R)
        ones_r = sb("ones_r", [P, P], F32R)
        w = sb("w", [P, 2, DC, W2], F32R)
        rows2 = sb("rows2", [P, 2, 2 * D], F32)
        norms = sb("norms", [P, PAIRS], F32)
        small = sb("small", [P, 8], F32)
        exponent = sb("exponent", [P, 1], U32)
        x_rows = sb("x_rows", [P, 2, D], F32)
        x_t = sb("x_t", [P, 2, 2, D], F32R)
        keys = sb("keys", [P, 2, 2, D], F16)
        turned_x = ps("turned_x", [P, 2, BANK], F32)
        p_values = ps("p_values", [P, 2, BANK], F32)
        p_keys = ps("p_keys", [P, 2, BANK], F32)
        p_turned_k = ps("p_turned_k", [P, 2, BANK], F32)
        column_norms = p_turned_k
        turned_k = p_turned_k[:].bitcast(F16).rearrange("p b (h c q) -> p b h c q", h=2, c=DC)

        with nc.Block() as block:
            @block.sync
            def _(sp):
                def load_x(t, b):
                    if from_tile(t, 2):
                        sp.wait_ge(x_turned, t - 1)
                    sp.dma_start(x_rows[:, b], x_in[bass.ds(t * P, P), :]).then_inc(x_loaded[b], 16)

                if layer == 0:
                    load_weights(sp, w_stack, 0, w_raw, w_loaded)
                load_x(0, 0)
                load_x(1, 1)
                if layer == 0:
                    pairs = x_in.rearrange("(j p two) d -> j p (two d)", p=P, two=2)
                    for j in range(PAIRS):
                        if j >= 2:
                            sp.wait_ge(norms_done, j - 1)
                        sp.dma_start(rows2[:, j % 2], pairs[j]).then_inc(norms_loaded[j % 2], 16)
                for t, b in row_tiles(sp, T):
                    if from_tile(t, 2):
                        load_x(t, b)

            @block.gpsimd
            def _(pool):
                pool.wait_ge(norm_ready, 1)
                pool.partition_all_reduce(small[:, 1:2], row_norm[:], P, REDUCE_MAX).then_inc(all_norm, 1)

            @block.scalar
            def _(act):
                def halve_x(t, b):
                    act.wait_ge(x_turned, t + 1)
                    if from_tile(t, 2):
                        act.wait_ge(keys_done, t - 1)
                    act.activation(x_t[:, b, HI], turned_x[:, b], ACT.Copy).then_inc(x_hi, 1)

                act.wait_ge(w_loaded, 16 * (layer + 1))
                act.activation(w_sq[:], w_raw[:], ACT.Square).then_inc(squared, 1)
                halve_x(0, 0)
                halve_x(1, 1)
                if layer == 0:
                    for j in range(PAIRS):
                        act.wait_ge(norms_loaded[j % 2], 16 * (j // 2 + 1))
                        act.activation(rows2[:, j % 2], rows2[:, j % 2], ACT.Square,
                                       accum_out=norms[:, j:j + 1]).then_inc(norms_done, 1)

                act.wait_ge(bound_ready, 1)
                act.activation(small[:, 3:4], small[:, 2:3], ACT.Sqrt).then_inc(root_ready, 1)
                for t, b in row_tiles(act, T):
                    if before_end(t, 1, T) and from_tile(t, 1):
                        halve_x(t + 1, 1 - b)
                    act.wait_ge(values_done, t + 1)
                    act.wait_ge(scale_ready, 1)
                    act.activation(values[:, HI, bass.ds(t, 1), :], p_values[:, b:b + 1], ACT.Copy,
                                   scale=scales[:, SCALE:SCALE + 1]).then_inc(values_hi, 1)
                    act.wait_ge(keys_done, t + 1)
                    if from_tile(t, 2):
                        act.wait_ge(keys_turned, t - 1)
                    act.activation(keys[:, b, HI], p_keys[:, b], ACT.Copy,
                                   scale=scales[:, SCALE:SCALE + 1]).then_inc(keys_hi, 1)

            @block.vector
            def _(dve):
                chain = Chain(dve, own)

                def halve_x(t, b):
                    dve.wait_ge(x_hi, t + 1)
                    dve.tensor_tensor(x_t[:, b, LO], turned_x[:, b], x_t[:, b, HI].bitcast(F32),
                                      ALU.subtract).then_inc(x_lo, 1)

                dve.tensor_copy(ones_r[:], ones[:]).then_inc(ones_made, 1)
                dve.wait_ge(w_loaded, 16 * (layer + 1))
                for c in range(DC):
                    dve.tensor_copy(w[:, HI, c], w_raw[:, c]).then_inc(w_split, 1)
                    dve.wait_ge(w_split, 2 * c + 1)
                    dve.tensor_tensor(w[:, LO, c], w_raw[:, c], w[:, HI, c].bitcast(F32),
                                      ALU.subtract).then_inc(w_split, 1)
                halve_x(0, 0)
                halve_x(1, 1)
                if layer == 0:
                    dve.wait_ge(norms_done, PAIRS)
                    chain.link(dve.reduce_max(row_norm[:], norms[:], AX_X))
                dve.tensor_copy(small[:, 4:5], row_norm[:]).then_inc(norm_ready, 1)
                dve.wait_ge(columns_done, 1)
                chain.link(dve.reduce_max(small[:, 0:1], column_norms[:].rearrange("p a b -> p (a b)"), AX_X))
                dve.wait_ge(all_norm, 1)
                chain.link(dve.tensor_tensor(small[:, 5:6], small[:, 0:1], small[:, 1:2], ALU.mult))
                dve.tensor_scalar(small[:, 2:3], small[:, 5:6], LEAST_BOUND, None, ALU.max).then_inc(bound_ready, 1)
                chain.link(dve.memset(exponent[:], EXPONENT_BITS))
                dve.wait_ge(root_ready, 1)
                chain.link(dve.reciprocal(small[:, 6:7], small[:, 3:4]))
                chain.link(dve.tensor_scalar(small[:, 7:8], small[:, 6:7], TOP, None, ALU.mult))
                chain.link(dve.tensor_tensor(scales[:, SCALE:SCALE + 1].bitcast(U32),
                                             small[:, 7:8].bitcast(U32), exponent[:], ALU.bitwise_and))
                chain.link(dve.reciprocal(small[:, 6:7], scales[:, SCALE:SCALE + 1]))
                chain.link(dve.tensor_tensor(scales[:, KEY_SCALE_INV2:KEY_SCALE_INV2 + 1],
                                             small[:, 6:7], small[:, 6:7], ALU.mult))
                chain.link(dve.tensor_scalar(scales[:, NEG_INV2:NEG_INV2 + 1],
                                             scales[:, KEY_SCALE_INV2:KEY_SCALE_INV2 + 1], -1.0, None, ALU.mult))
                dve.tensor_scalar(scales[:, OUT_SCALE:OUT_SCALE + 1], small[:, 6:7],
                                  1.0 / PROB_SCALE, None, ALU.mult).then_inc(scale_ready, 1)
                scale = scales[:, SCALE:SCALE + 1]

                def store_keys(t, b):
                    dve.wait_ge(keys_turned, t + 1)
                    dve.tensor_scalar(keys_t[:, :, :, bass.ds(t * P, P)], turned_k[:, b], 1.0, None,
                                      ALU.mult).then_inc(keys_stored, 1)

                for t, b in row_tiles(dve, T):
                    if before_end(t, 1, T) and from_tile(t, 1):
                        halve_x(t + 1, 1 - b)
                    if from_tile(t, 1):
                        store_keys(t - 1, 1 - b)
                    dve.wait_ge(values_hi, t + 1)
                    dve.scalar_tensor_tensor(out=values[:, LO, bass.ds(t, 1), :], in0=p_values[:, b:b + 1],
                                             scalar=scale, in1=values[:, HI, bass.ds(t, 1), :],
                                             op0=ALU.mult, op1=ALU.subtract).then_inc(values_lo, 1)
                    dve.wait_ge(keys_hi, t + 1)
                    dve.scalar_tensor_tensor(out=keys[:, b, LO], in0=p_keys[:, b], scalar=scale,
                                             in1=keys[:, b, HI], op0=ALU.mult,
                                             op1=ALU.subtract).then_inc(keys_lo, 1)
                store_keys(T - 1, (T - 1) % 2)

            @block.tensor
            def _(pe):
                def turn_x(t, b):
                    pe.wait_ge(x_loaded[b], landed(t, b))
                    if from_tile(t, 2):
                        pe.wait_ge(x_lo, t - 1)
                    for c in range(DC):
                        last = pe.transpose(turned_x[:, b, c * P:(c + 1) * P],
                                            x_rows[:, b, c * P:(c + 1) * P], ident[:])
                    last.then_inc(x_turned, 1)

                def product(bank, t, b, columns):
                    parts = [(HI, HI), (HI, LO), (LO, HI)]
                    for c in range(DC):
                        if fixed(t) and t == 0:
                            pe.wait_ge(w_split, 2 * (c + 1))
                        for n, (xh, wh) in enumerate(parts):
                            last = pe.matmul(bank, x_t[:, b, xh, c * P:(c + 1) * P], w[:, wh, c, columns],
                                             start=(c == 0 and n == 0), stop=(c == DC - 1 and n == 2))
                    return last

                def turn_keys(t, b):
                    pe.wait_ge(keys_lo, t + 1)
                    if from_tile(t, 2):
                        pe.wait_ge(keys_stored, t - 1)
                    for half in (HI, LO):
                        for c in range(DC):
                            last = pe.transpose(turned_k[:, b, half, c, :],
                                                keys[:, b, half, c * P:(c + 1) * P], ident16[:])
                    last.then_inc(keys_turned, 1)

                turn_x(0, 0)
                turn_x(1, 1)
                pe.wait_ge(squared, 1)
                pe.wait_ge(ones_made, 1)
                for half in range(W2 // BANK):
                    for c in range(DC):
                        last = pe.matmul(column_norms[:, half], ones_r[:],
                                         w_sq[:, c, half * BANK:(half + 1) * BANK],
                                         start=(c == 0), stop=(c == DC - 1))
                last.then_inc(columns_done, 1)
                for t, b in row_tiles(pe, T):
                    if before_end(t, 1, T) and from_tile(t, 1):
                        turn_x(t + 1, 1 - b)
                    pe.wait_ge(x_lo, t + 1)
                    if from_tile(t, 2):
                        pe.wait_ge(values_lo, t - 1)
                    product(p_values[:, b], t, b, slice(0, D)).then_inc(values_done, 1)
                    if from_tile(t, 1):
                        turn_keys(t - 1, 1 - b)
                    if from_tile(t, 2):
                        pe.wait_ge(keys_lo, t - 1)
                    product(p_keys[:, b], t, b, slice(D, 2 * D)).then_inc(keys_done, 1)
                turn_keys(T - 1, (T - 1) % 2)


def attend(nc, sem, layer, x_in, x_first, adj, rows_out, kept, values, keys_t,
           w_stack, w_raw, w_loaded, N, NP, T, DC, D, last_layer):
    ident, ident16, ones, scales = kept["ident"], kept["ident16"], kept["ones"], kept["scales"]
    row_norm, var_eps = kept["row_norm"], kept["var_eps"]
    first_layer = layer == 0
    KC = ceil_div(NP, BANK)
    widths = [min(BANK, NP - k * BANK) for k in range(KC)]
    valid = [min(BANK, N - k * BANK) for k in range(KC)]
    PART = NP // PARTS
    GROUP = BANK // P
    G = ceil_div(T, GROUP)
    members = [range(g * GROUP, min(T, (g + 1) * GROUP)) for g in range(G)]
    SLOTS = 4
    LINKS = 9 if last_layer else 6

    def named(name):
        return sem(f"{name}_a{layer}")

    adj_loaded, x_loaded, stored = (
        [named(f"{n}{b}") for b in (0, 1)] for n in ("adj_loaded", "x_loaded", "stored"))
    q_staged, q_turned, q_ready = (named(n) for n in ("q_staged", "q_turned", "q_ready"))
    scores_done, scores_read, shift_ready = (named(n) for n in ("scores_done", "scores_read", "shift_ready"))
    exp_done, masked, pad_zeroed = (named(n) for n in ("exp_done", "masked", "pad_zeroed"))
    probs_turned, probs_hi, probs_split, mixed = (
        named(n) for n in ("probs_turned", "probs_hi", "probs_split", "mixed"))
    adj_anded, adj_checked, adj_low = named("adj_anded"), named("adj_checked"), kept["adj_low"]
    rows_done, own, peak_own = (named(n) for n in ("rows_done", "dve_chain", "peak_chain"))

    with ExitStack() as s:
        def sb(name, shape, dt):
            return s.enter_context(nc.sbuf_tensor(f"{name}_a{layer}", shape, dt))

        def ps(name, shape, dt):
            return s.enter_context(nc.psum_tensor(f"{name}_a{layer}", shape, dt))

        row = sb("row", [P, 2, NP], F32)
        adj_row = sb("adj_row", [P, 2, NP], F32)
        probs = sb("probs", [P, SLOTS, 2, GROUP * P], F16)
        q_rows = sb("q_rows", [P, 2, D], F16)
        q_t = sb("q_t", [P, 2, 2, DC, P], F16)
        peaks = sb("peaks", [P, 2, KC + 1], F32)
        shift = sb("shift", [P, 2], F32)
        sums = sb("sums", [P, 2, PARTS], F32)
        small = sb("small", [P, 16], F32)
        stats = sb("stats", [P, 8], F32)
        waited = sb("waited", [P, 1], F32)
        x_rows = sb("x_rows", [P, 2, D], F32)
        x0_rows = sb("x0_rows", [P, 2, D], F32) if last_layer else None
        work = sb("work", [P, 2, D], F32)
        y_rows = sb("y_rows", [P, 2, D], F32)
        low_words = sb("low_words", [P, PART], U32) if first_layer else None
        p_scores = ps("p_scores", [P, 2, BANK], F32)
        p_probs = ps("p_probs", [P, 2, BANK], F32)
        p_out = ps("p_out", [P, 2, BANK], F32)
        p_q = ps("p_q", [P, 2, DC, P], F16)
        X_LOADS = 2 if last_layer else 1

        with nc.Block() as block:
            @block.sync
            def _(sp):
                def store(t, b):
                    sp.dma_start(rows_out[bass.ds(t * P, P), :], y_rows[:, b]).then_inc(stored[b], 16)

                for t, b in row_tiles(sp, T):
                    if from_tile(t, 2):
                        sp.wait_ge(masked, PARTS * (t - 1))
                        if first_layer:
                            sp.wait_ge(adj_checked, PARTS * (t - 1))
                    if fixed(t) and t == 1 and not last_layer:
                        load_weights(sp, w_stack, layer + 1, w_raw, w_loaded)
                    sp.dma_start(adj_row[:, b], adj[bass.ds(t * P, P), :]).then_inc(adj_loaded[b], 16)
                    if from_tile(t, 2):
                        sp.wait_ge(rows_done, t - 1)
                        store(t - 2, b)
                    sp.dma_start(x_rows[:, b], x_in[bass.ds(t * P, P), :]).then_inc(x_loaded[b], 16)
                    if last_layer:
                        sp.dma_start(x0_rows[:, b], x_first[bass.ds(t * P, P), :]).then_inc(x_loaded[b], 16)
                for t in (T - 2, T - 1):
                    sp.wait_ge(rows_done, t + 1)
                    store(t, t % 2)
                for b in (0, 1):
                    sp.wait_ge(stored[b], 16 * (T // 2))

            @block.tensor
            def _(pe):
                def turn_q(t):
                    pe.wait_ge(q_staged, t + 1)
                    if from_tile(t, 1):
                        pe.wait_ge(q_ready, t)
                    for half in (HI, LO):
                        for c in range(DC):
                            last = pe.transpose(p_q[:, half, c, :], q_rows[:, half, c * P:(c + 1) * P], ident16[:])
                    last.then_inc(q_turned, 1)

                def scores(t, b, chunks):
                    pe.wait_ge(q_ready, t + 1)
                    for k in chunks:
                        bank = (b * KC + k) % 2
                        if from_tile(t, 1) or k >= 2:
                            pe.wait_ge(scores_read, t * KC + k - 1)
                        n = 0
                        for c in range(DC):
                            for qh, kh in ((HI, HI), (HI, LO), (LO, HI)):
                                last = pe.matmul(p_scores[:, bank, 0:widths[k]], q_t[:, b, qh, c, :],
                                                 keys_t[:, kh, c, k * BANK:k * BANK + widths[k]],
                                                 start=(n == 0), stop=(n == 3 * DC - 1))
                                n += 1
                        last.then_inc(scores_done, 1)

                def turn_probs(t, b, g):
                    if from_tile(t, 1) or g >= 2:
                        pe.wait_ge(probs_split, t * G + g - 1)
                    for j, k in enumerate(members[g]):
                        last = pe.transpose(p_probs[:, (b * G + g) % 2, j * P:(j + 1) * P],
                                            row[:, b, k * P:(k + 1) * P], ident[:])
                    last.then_inc(probs_turned, 1)

                def mix(t, b, g):
                    pe.wait_ge(probs_split, t * G + g + 1)
                    for j, k in enumerate(members[g]):
                        for n, (ph, vh) in enumerate(((HI, HI), (HI, LO), (LO, HI))):
                            last = pe.matmul(p_out[:, b], probs[:, g % SLOTS, ph, j * P:(j + 1) * P], values[:, vh, k, :],
                                             start=(k == 0 and n == 0), stop=(k == T - 1 and n == 2))
                    last.then_inc(mixed, 1)

                turn_q(0)
                turn_q(1)
                scores(0, 0, range(KC))
                for t, b in row_tiles(pe, T):
                    if before_end(t, 1, T):
                        scores(t + 1, 1 - b, range(KC - 1))
                    pe.wait_ge(masked, PARTS * (t + 1))
                    turn_probs(t, b, 0)
                    turn_probs(t, b, 1)
                    if before_end(t, 1, T):
                        scores(t + 1, 1 - b, range(KC - 1, KC))
                    if before_end(t, 2, T):
                        turn_q(t + 2)
                    if from_tile(t, 2):
                        pe.wait_ge(rows_done, t - 1)
                    for g in range(G):
                        mix(t, b, g)
                        if g + 2 < G:
                            turn_probs(t, b, g + 2)

            @block.scalar
            def _(act):
                def exp_part(t, b, part):
                    if part == 0:
                        if from_tile(t, 2):
                            act.wait_ge(rows_done, t - 1)
                        act.wait_ge(shift_ready, t + 1)
                    piece = row[:, b, part * PART:min(N, (part + 1) * PART)]
                    act.activation(piece, piece, ACT.Exp, bias=shift[:, b:b + 1],
                                   scale=scales[:, KEY_SCALE_INV2:KEY_SCALE_INV2 + 1],
                                   accum_out=sums[:, b, part:part + 1]).then_inc(exp_done, 1)

                for part in range(PARTS):
                    exp_part(0, 0, part)
                for t, b in row_tiles(act, T):
                    for g in range(G):
                        act.wait_ge(probs_turned, t * G + g + 1)
                        used = len(members[g]) * P
                        act.activation(probs[:, g % SLOTS, HI, 0:used], p_probs[:, (b * G + g) % 2, 0:used],
                                       ACT.Copy, scale=PROB_SCALE).then_inc(probs_hi, 1)
                        if 1 <= g <= PARTS and before_end(t, 1, T):
                            exp_part(t + 1, 1 - b, g - 1)

            @block.gpsimd
            def _(pool):
                for t, b in row_tiles(pool, T):
                    pool.wait_ge(adj_loaded[b], landed(t, b))
                    pool.wait_ge(pad_zeroed, 2)
                    for part in range(PARTS):
                        pool.wait_ge(exp_done, t * PARTS + part + 1)
                        piece = slice(part * PART, (part + 1) * PART)
                        pool.tensor_tensor(row[:, b, piece], row[:, b, piece], adj_row[:, b, piece],
                                           ALU.mult).then_inc(masked, 1)

            @block.vector
            def _(dve):
                peak_chain, chain = Chain(dve, peak_own, 1), Chain(dve, own, LINKS)

                def stage_q(t):
                    if from_tile(t, 1):
                        dve.wait_ge(q_turned, t)
                    dve.tensor_scalar(q_rows[:].rearrange("p (h o) d -> p h o d", o=1),
                                      values[:, :, bass.ds(t, 1), :], 1.0, None, ALU.mult).then_inc(q_staged, 1)

                def copy_q(t, b):
                    dve.wait_ge(q_turned, t + 1)
                    if from_tile(t, 2):
                        dve.wait_ge(scores_done, (t - 1) * KC)
                    dve.tensor_copy(q_t[:, b], p_q[:]).then_inc(q_ready, 1)

                def read_scores(t, b, k):
                    if k == 0 and from_tile(t, 2):
                        dve.wait_ge(probs_turned, (t - 1) * G)
                    dve.wait_ge(scores_done, t * KC + k + 1)
                    dve.wait_ge(pad_zeroed, 2)
                    w = valid[k]
                    dve.tensor_scalar(row[:, b, k * BANK:k * BANK + w], p_scores[:, (b * KC + k) % 2, 0:w],
                                      1.0, LOWEST, ALU.mult, ALU.max,
                                      accum_out=peaks[:, b, k:k + 1]).then_inc(scores_read, 1)

                def make_shift(t, b):
                    peak_chain.tile(t)
                    dve.wait_ge(scores_read, (t + 1) * KC)
                    peak_chain.link(dve.reduce_max(peaks[:, b, KC:KC + 1], peaks[:, b, 0:KC], AX_X))
                    dve.tensor_tensor(shift[:, b:b + 1], peaks[:, b, KC:KC + 1],
                                      scales[:, NEG_INV2:NEG_INV2 + 1], ALU.mult).then_inc(shift_ready, 1)

                def split_probs(t, b, g):
                    dve.wait_ge(probs_hi, t * G + g + 1)
                    used = len(members[g]) * P
                    dve.scalar_tensor_tensor(out=probs[:, g % SLOTS, LO, 0:used], in0=p_probs[:, (b * G + g) % 2, 0:used],
                                             scalar=PROB_SCALE, in1=probs[:, g % SLOTS, HI, 0:used],
                                             op0=ALU.mult, op1=ALU.subtract).then_inc(probs_split, 1)

                def finish(t, b):
                    chain.tile(t)
                    r = small[:, 8 * b:8 * b + 8]
                    dve.wait_ge(mixed, (t + 1) * G)
                    chain.link(dve.reduce_sum(r[:, 0:1], sums[:, b], AX_X))
                    chain.link(dve.reciprocal(r[:, 1:2], r[:, 0:1]))
                    chain.link(dve.tensor_tensor(r[:, 2:3], r[:, 1:2], scales[:, OUT_SCALE:OUT_SCALE + 1], ALU.mult))
                    dve.wait_ge(x_loaded[b], landed(t, b, X_LOADS))
                    chain.link(dve.scalar_tensor_tensor(out=work[:, b], in0=p_out[:, b], scalar=r[:, 2:3],
                                                        in1=x_rows[:, b], op0=ALU.mult, op1=ALU.add))
                    if from_tile(t, 2):
                        dve.wait_ge(stored[b], landed(t - 2, b))
                    if not last_layer:
                        chain.link(dve.scalar_tensor_tensor(out=y_rows[:, b], in0=work[:, b], scalar=SLOPE,
                                                            in1=work[:, b], op0=ALU.mult, op1=ALU.max))
                        chain.link(dve.tensor_tensor_reduce(work[:, b], y_rows[:, b], y_rows[:, b], 1.0, 0.0,
                                                            ALU.mult, ALU.add, r[:, 3:4]))
                        dve.tensor_tensor(row_norm[:], row_norm[:], r[:, 3:4], ALU.max).then_inc(rows_done, 1)
                    else:
                        chain.link(dve.scalar_tensor_tensor(out=y_rows[:, b], in0=work[:, b], scalar=SLOPE,
                                                            in1=work[:, b], op0=ALU.mult, op1=ALU.max))
                        chain.link(dve.tensor_tensor(work[:, b], y_rows[:, b], x0_rows[:, b], ALU.add))
                        chain.link(dve.bn_stats(stats[:, 0:6], work[:, b]))
                        dve.memset(waited[:], 0.0)
                        chain.link(dve.bn_aggr(stats[:, 6:8], stats[:, 0:6]))
                        chain.link(dve.tensor_scalar(var_eps[:, bass.ds(t, 1)], stats[:, 7:8], EPS, None, ALU.add))
                        dve.tensor_scalar(y_rows[:, b], work[:, b], stats[:, 6:7], None,
                                          ALU.subtract).then_inc(rows_done, 1)
                    assert chain.done == LINKS

                def check_adj(t, b, part):
                    dve.wait_ge(adj_loaded[b], landed(t, b))
                    if from_tile(t, 1) or part > 0:
                        dve.wait_ge(adj_checked, t * PARTS + part)
                    dve.tensor_scalar(low_words[:], adj_row[:, b, part * PART:(part + 1) * PART].bitcast(U32),
                                      LOW_BITS, None, ALU.bitwise_and).then_inc(adj_anded, 1)
                    dve.wait_ge(adj_anded, t * PARTS + part + 1)
                    dve.wait_ge(pad_zeroed, 2)
                    dve.reduce_max(adj_low[:, bass.ds(t * PARTS + part, 1)], low_words[:],
                                   AX_X).then_inc(adj_checked, 1)

                for b in (0, 1):
                    dve.memset(row[:, b, N:NP], 0.0).then_inc(pad_zeroed, 1)
                stage_q(0)
                copy_q(0, 0)
                stage_q(1)
                copy_q(1, 1)
                for k in range(KC):
                    read_scores(0, 0, k)
                make_shift(0, 0)
                if first_layer:
                    for part in range(PARTS):
                        check_adj(0, 0, part)
                for t, b in row_tiles(dve, T):
                    ahead = before_end(t, 1, T)
                    if ahead:
                        read_scores(t + 1, 1 - b, 0)
                    if from_tile(t, 1):
                        finish(t - 1, 1 - b)
                    if ahead:
                        for k in range(1, KC - 1):
                            read_scores(t + 1, 1 - b, k)
                    if before_end(t, 2, T):
                        stage_q(t + 2)
                    split_probs(t, b, 0)
                    split_probs(t, b, 1)
                    if ahead:
                        read_scores(t + 1, 1 - b, KC - 1)
                        make_shift(t + 1, 1 - b)
                    if before_end(t, 2, T):
                        copy_q(t + 2, b)
                    for g in range(2, G):
                        split_probs(t, b, g)
                        if first_layer and ahead and g - 2 < PARTS:
                            check_adj(t + 1, 1 - b, g - 2)
                finish(T - 1, (T - 1) % 2)


def binary_layer(nc, sem, centred, weight, adj_t, out, kept, T, DC, D):
    ident, ident16, var_eps, adj_low = (kept[n] for n in ("ident", "ident16", "var_eps", "adj_low"))
    names = ("weight_loaded", "weight_turned", "signs_made", "above", "rows_turned", "rows_copied",
             "products_done", "products_kept", "roots", "rstd_made", "low_bits_found", "low_bits_max",
             "low_bits_ready", "adj_hi_made", "adj_lo_made", "sums_done", "var_made", "std_made",
             "rows_done", "dve_chain")
    (weight_loaded, weight_turned, signs_made, above, rows_turned, rows_copied,
     products_done, products_kept, roots, rstd_made, low_bits_found, low_bits_max,
     low_bits_ready, adj_hi_made, adj_lo_made, sums_done, var_made, std_made,
     rows_done, own) = (sem(f"{n}_b") for n in names)
    rows_loaded, adj_loaded, y_loaded, stored = (
        [sem(f"{n}{b}_b") for b in (0, 1)] for n in ("rows_loaded", "adj_loaded", "y_loaded", "stored"))
    LINKS = 5

    with ExitStack() as s:
        def sb(name, shape, dt):
            return s.enter_context(nc.sbuf_tensor(f"{name}_b", shape, dt))

        def ps(name, shape, dt):
            return s.enter_context(nc.psum_tensor(f"{name}_b", shape, dt))

        products = sb("products", [P, T, D], F32R)
        w_rows = sb("w_rows", [P, DC, D], F32)
        positive = sb("positive", [P, DC, D], F16)
        negative = sb("negative", [P, DC, D], F16)
        signs_t = sb("signs_t", [P, DC, D], F16)
        rows = sb("rows", [P, 2, D], F32)
        bits = sb("bits", [P, 2, D], F16)
        bits_t = sb("bits_t", [P, 2, DC * P], F16)
        root = sb("root", [P, T], F32)
        rstd = sb("rstd", [P, T], F32)
        flag = sb("flag", [P, 2], F32)
        has_low = sb("has_low", [P, 1], mybir.dt.int32)
        adj_raw = sb("adj_raw", [P, 2, T * P], F32)
        adj_hi = sb("adj_hi", [P, 2, T * P], F32R)
        adj_lo = sb("adj_lo", [P, 2, T * P], F32R)
        y_in = sb("y_in", [P, 2, D], F32)
        work = sb("work", [P, 2, D], F32)
        y_rows = sb("y_rows", [P, 2, D], F32)
        stats = sb("stats", [P, 2, 8], F32)
        std = sb("std", [P, 2, 4], F32)
        waited = sb("waited", [P, 1], F32)
        p_w = ps("p_w", [P, DC, BANK], F32)
        p_bits = ps("p_bits", [P, 2, 2 * BANK], F16)
        p_out = ps("p_out", [P, 2, BANK], F32)

        def by_low_bits(engine, body):
            engine.wait_ge(low_bits_ready, 1)
            low = engine.value_load(has_low[0:1, 0:1], min_val=0, max_val=LOW_BITS)
            with engine.If(low > 0):
                body(True)
            with engine.Else():
                body(False)

        with nc.Block() as block:
            @block.sync
            def _(sp):
                def load_adj(t, b):
                    sp.dma_start(adj_raw[:, b], adj_t[bass.ds(t * P, P), :]).then_inc(adj_loaded[b], 16)

                def load_y(t, b):
                    sp.dma_start(y_in[:, b], centred[bass.ds(t * P, P), :]).then_inc(y_loaded[b], 16)

                def store(t, b):
                    sp.dma_start(out[bass.ds(t * P, P), :], y_rows[:, b]).then_inc(stored[b], 16)

                sp.dma_start(w_rows[:], weight.rearrange("(r p) n -> p r n", p=P)).then_inc(weight_loaded, 16)
                for t, b in row_tiles(sp, T):
                    if from_tile(t, 2):
                        sp.wait_ge(above, t - 1)
                    sp.dma_start(rows[:, b], centred[bass.ds(t * P, P), :]).then_inc(rows_loaded[b], 16)
                for t in (0, 1):
                    load_adj(t, t)
                    load_y(t, t)

                def tiles_of(split):
                    for t, b in row_tiles(sp, T):
                        if from_tile(t, 2):
                            sp.wait_ge(adj_lo_made if split else adj_hi_made, t - 1)
                            load_adj(t, b)
                            sp.wait_ge(rows_done, t - 1)
                            store(t - 2, b)
                            load_y(t, b)
                    for t in (T - 2, T - 1):
                        sp.wait_ge(rows_done, t + 1)
                        store(t, t % 2)

                by_low_bits(sp, tiles_of)
                for b in (0, 1):
                    sp.wait_ge(stored[b], 16 * (T // 2))

            @block.gpsimd
            def _(pool):
                pool.wait_ge(low_bits_found, 1)
                pool.partition_all_reduce(flag[:, 1:2], flag[:, 0:1], P, REDUCE_MAX).then_inc(low_bits_max, 1)

            @block.tensor
            def _(pe):
                pe.wait_ge(weight_loaded, 16)
                for c in range(DC):
                    for r in range(DC):
                        last = pe.transpose(p_w[:, c, r * P:(r + 1) * P], w_rows[:, r, c * P:(c + 1) * P], ident[:])
                last.then_inc(weight_turned, 1)

                def turn(t, b):
                    pe.wait_ge(above, t + 1)
                    if from_tile(t, 2):
                        pe.wait_ge(rows_copied, t - 1)
                    for c in range(DC):
                        last = pe.transpose(p_bits[:, b, c * P:(c + 1) * P], bits[:, b, c * P:(c + 1) * P], ident16[:])
                    last.then_inc(rows_turned, 1)

                turn(0, 0)
                turn(1, 1)
                pe.wait_ge(signs_made, 3)
                for t, b in row_tiles(pe, T):
                    pe.wait_ge(rows_copied, t + 1)
                    if before_end(t, 2, T):
                        turn(t + 2, b)
                    if from_tile(t, 2):
                        pe.wait_ge(products_kept, t - 1)
                    for c in range(DC):
                        last = pe.matmul(p_out[:, b], bits_t[:, b, c * P:(c + 1) * P], signs_t[:, c],
                                         start=(c == 0), stop=(c == DC - 1))
                    last.then_inc(products_done, 1)
                pe.wait_ge(products_kept, T)

                def tiles_of(split):
                    halves = (adj_hi, adj_lo) if split else (adj_hi,)
                    for t, b in row_tiles(pe, T):
                        pe.wait_ge(adj_lo_made if split else adj_hi_made, t + 1)
                        if from_tile(t, 2):
                            pe.wait_ge(rows_done, t - 1)
                        for k in range(T):
                            for half in halves:
                                last = pe.matmul(p_out[:, b], half[:, b, k * P:(k + 1) * P], products[:, k, :],
                                                 start=(k == 0 and half is adj_hi),
                                                 stop=(k == T - 1 and half is halves[-1]))
                        last.then_inc(sums_done, 1)

                by_low_bits(pe, tiles_of)

            @block.scalar
            def _(act):
                act.activation(root[:], var_eps[:], ACT.Sqrt).then_inc(roots, 1)
                for t, b in row_tiles(act, T):
                    act.wait_ge(rows_turned, t + 1)
                    if from_tile(t, 2):
                        act.wait_ge(products_done, t - 1)
                    act.activation(bits_t[:, b], p_bits[:, b, 0:DC * P], ACT.Copy).then_inc(rows_copied, 1)

                def copy_hi(t, b):
                    act.wait_ge(adj_loaded[b], landed(t, b))
                    if from_tile(t, 2):
                        act.wait_ge(sums_done, t - 1)
                    act.activation(adj_hi[:, b], adj_raw[:, b], ACT.Copy).then_inc(adj_hi_made, 1)

                copy_hi(0, 0)

                def tiles_of(split):
                    for t, b in row_tiles(act, T):
                        if before_end(t, 1, T):
                            copy_hi(t + 1, 1 - b)
                        act.wait_ge(var_made, t + 1)
                        act.activation(std[:, b, 1:2], std[:, b, 0:1], ACT.Sqrt).then_inc(std_made, 1)

                by_low_bits(act, tiles_of)

            @block.vector
            def _(dve):
                def compare(t, b):
                    dve.wait_ge(rows_loaded[b], landed(t, b))
                    if from_tile(t, 2):
                        dve.wait_ge(rows_turned, t - 1)
                    dve.tensor_scalar(bits[:, b], rows[:, b], 0.0, None, ALU.is_gt).then_inc(above, 1)

                dve.wait_ge(weight_turned, 1)
                dve.tensor_scalar(positive[:], p_w[:], 0.0, None, ALU.is_gt).then_inc(signs_made, 1)
                dve.tensor_scalar(negative[:], p_w[:], 0.0, None, ALU.is_lt).then_inc(signs_made, 1)
                compare(0, 0)
                compare(1, 1)
                dve.wait_ge(signs_made, 2)
                dve.tensor_tensor(signs_t[:], positive[:], negative[:], ALU.subtract).then_inc(signs_made, 1)
                dve.reduce_max(flag[:, 0:1], adj_low[:], AX_X).then_inc(low_bits_found, 1)
                dve.wait_ge(roots, 1)
                dve.reciprocal(rstd[:], root[:]).then_inc(rstd_made, 1)
                for t, b in row_tiles(dve, T):
                    if before_end(t, 2, T):
                        compare(t + 2, b)
                    dve.wait_ge(products_done, t + 1)
                    dve.tensor_scalar(products[:, bass.ds(t, 1), :], p_out[:, b:b + 1], 1.0, None,
                                      ALU.mult).then_inc(products_kept, 1)
                dve.wait_ge(low_bits_max, 1)
                dve.tensor_copy(has_low[:], flag[:, 1:2]).then_inc(low_bits_ready, 1)
                dve.wait_ge(rstd_made, 1)

                def make_lo(t, b):
                    dve.wait_ge(adj_hi_made, t + 1)
                    dve.tensor_tensor(adj_lo[:, b], adj_raw[:, b], adj_hi[:, b].bitcast(F32),
                                      ALU.subtract).then_inc(adj_lo_made, 1)

                def tiles_of(split):
                    chain = Chain(dve, own, LINKS)
                    if split:
                        make_lo(0, 0)
                    for t, b in row_tiles(dve, T):
                        if split and before_end(t, 1, T):
                            make_lo(t + 1, 1 - b)
                        chain.tile(t)
                        dve.wait_ge(y_loaded[b], landed(t, b))
                        chain.link(dve.tensor_scalar(work[:, b], y_in[:, b], rstd[:, bass.ds(t, 1)], None, ALU.mult))
                        dve.wait_ge(sums_done, t + 1)
                        chain.link(dve.scalar_tensor_tensor(out=work[:, b], in0=p_out[:, b], scalar=0.0,
                                                            in1=work[:, b], op0=ALU.max, op1=ALU.add))
                        chain.link(dve.bn_stats(stats[:, b, 0:6], work[:, b]))
                        dve.memset(waited[:], 0.0)
                        chain.link(dve.bn_aggr(stats[:, b, 6:8], stats[:, b, 0:6]))
                        dve.tensor_scalar(std[:, b, 0:1], stats[:, b, 7:8], EPS, None, ALU.add).then_inc(var_made, 1)
                        dve.wait_ge(std_made, t + 1)
                        chain.link(dve.reciprocal(std[:, b, 2:3], std[:, b, 1:2]))
                        if from_tile(t, 2):
                            dve.wait_ge(stored[b], landed(t - 2, b))
                        dve.tensor_scalar(y_rows[:, b], work[:, b], stats[:, b, 6:7], std[:, b, 2:3],
                                          ALU.subtract, ALU.mult).then_inc(rows_done, 1)
                        assert chain.done == LINKS

                by_low_bits(dve, tiles_of)


def kernel(x, adj, L0_gnn_W_stack, L1_gnn_weight):
    import numpy as np
    import concourse.bacc as bacc
    from concourse.bass_utils import run_bass_kernel_spmd

    x, adj = np.asarray(x), np.asarray(adj)
    n, d = x.shape
    padded = ceil_div(n, P) * P
    tiles = padded // P
    x_rows = np.zeros((padded, d), x.dtype)
    x_rows[:n] = x
    adj_rows = np.zeros((padded, padded), adj.dtype)
    adj_rows[:n, :n] = adj
    adj_blocks = np.ascontiguousarray(adj_rows.reshape(tiles, P, tiles, P).transpose(0, 3, 2, 1))
    arrays = {
        "x_rows": x_rows,
        "adj_rows": adj_rows,
        "adj_blocks": adj_blocks.reshape(padded, padded),
        "w_stack": np.ascontiguousarray(L0_gnn_W_stack),
        "weight": np.ascontiguousarray(L1_gnn_weight),
        "identity": np.eye(P, dtype=np.float32),
    }
    nc = bacc.Bacc("TRN2", target_bir_lowering=False, num_devices=1)
    aps = [nc.dram_tensor(name, a.shape, mybir.dt.from_np(a.dtype), kind="ExternalInput").ap()
           for name, a in arrays.items()]
    result = nc.dram_tensor("result", (padded, d), F32, kind="ExternalOutput").ap()
    build(nc, n, *aps, result)
    got = run_bass_kernel_spmd(nc, [arrays], core_ids=[0])
    return got.results[0]["result"][:n]
```

```python
from contextlib import ExitStack

import concourse.bass as bass
from concourse import mybir
from concourse.alu_op_type import AluOpType as ALU

ACT = mybir.ActivationFunctionType
F32 = mybir.dt.float32
F32R = mybir.dt.float32r
F16 = mybir.dt.float16
BF16 = mybir.dt.bfloat16
U32 = mybir.dt.uint32
AX_X = mybir.AxisListType.X
REDUCE_MAX = bass.bass_isa.ReduceOp.max

P = 128
HI, LO = 0, 1
BANK = 512
SLOPE = 0.01
EPS = 1e-5
PARTS = 4
PROB_SCALE = 1024.0
TOP = 2.0 ** 14
LOWEST = -3.0e38
LEAST_BOUND = 1e-30
LOW_BITS = 0xFFFF
EXPONENT_BITS = 0x7F800000


def ceil_div(a, b):
    return -(-a // b)


def row_tiles(engine, tiles):
    for t in (0, 1):
        yield t, t
    with engine.Fori(1, tiles // 2 - 1) as pair:
        for b in (0, 1):
            yield pair * 2 + b, b
    for t in (tiles - 2, tiles - 1):
        yield t, t % 2


def quad_tiles(engine, tiles):
    assert tiles % 4 == 2
    for t in range(4):
        yield t, t
    with engine.Fori(1, tiles // 4) as quad:
        for r in range(4):
            yield quad * 4 + r, r
    for t in (tiles - 2, tiles - 1):
        yield t, t % 4


def fixed(t):
    return isinstance(t, int)


def from_tile(t, first):
    return not fixed(t) or t >= first


def before_end(t, ahead, tiles):
    return not fixed(t) or t + ahead < tiles


def landed(t, b, transfers=1, ring=2):
    return (t - b) * (16 * transfers // ring) + 16 * transfers


class Chain:

    def __init__(self, engine, sem, per_tile=0):
        self.engine, self.sem, self.per_tile = engine, sem, per_tile
        self.base, self.done = 0, 0

    def tile(self, t):
        self.base, self.done = t * self.per_tile, 0

    def link(self, instruction):
        self.done += 1
        instruction.then_inc(self.sem, 1)
        self.engine.wait_ge(self.sem, self.base + self.done)


def build(nc, N, x, adj, adj_t, w_stack, weight, identity, out):
    NP, D = x.shape
    T = NP // P
    DC = D // P
    LAYERS = w_stack.shape[0]
    assert T % 2 == 0 and D == BANK

    with ExitStack() as whole:
        def sem(name):
            return whole.enter_context(nc.semaphore(name))

        def keep(name, shape, dt):
            return whole.enter_context(nc.sbuf_tensor(name, shape, dt))

        kept = {
            "ident": keep("ident", [P, P], F32),
            "ident16": keep("ident16", [P, P], F16),
            "ones": keep("ones", [P, P], F32),
            "scales": keep("scales", [P, 8], F32),
            "row_norm": keep("row_norm", [P, 1], F32),
            "var_eps": keep("var_eps", [P, T], F32),
            "adj_low": keep("adj_low", [P, T * PARTS], F32),
        }
        x_mid = nc.dram_tensor("x_mid", [NP, D], F32, kind="Internal").ap()
        centred = nc.dram_tensor("centred", [NP, D], F32, kind="Internal").ap()
        adj_t16 = nc.dram_tensor("adj_t16", list(adj_t.shape), BF16, kind="Internal").ap()
        adj_cast = sem("adj_cast")

        constants(nc, sem, identity, kept)
        layer_in = x
        w_loaded = sem("w_loaded")
        with ExitStack() as layers:
            w_raw = layers.enter_context(nc.sbuf_tensor("w_raw", [P, DC, w_stack.shape[2]], F32))
            for layer in range(LAYERS):
                last = layer == LAYERS - 1
                layer_out = centred if last else x_mid
                with ExitStack() as s:
                    values = s.enter_context(nc.sbuf_tensor(f"values{layer}", [P, 2, T, D], F16))
                    keys_t = s.enter_context(nc.sbuf_tensor(f"keys_t{layer}", [P, 2, DC, NP], F16))
                    project(nc, sem, layer, layer_in, w_stack, w_raw, w_loaded, kept, values, keys_t, T, DC, D)
                    attend(nc, sem, layer, layer_in, x, adj, layer_out, kept, values, keys_t,
                           w_stack, w_raw, w_loaded, adj_t, adj_t16, adj_cast, N, NP, T, DC, D, last)
                layer_in = x_mid
        binary_layer(nc, sem, centred, weight, adj_t, adj_t16, out, kept, T, DC, D)


def constants(nc, sem, identity, kept):
    loaded, made = sem("identity_loaded"), sem("constants_made")
    with nc.Block() as block:
        @block.sync
        def _(sp):
            sp.dma_start(kept["ident"][:], identity).then_inc(loaded, 16)

        @block.vector
        def _(dve):
            dve.memset(kept["ones"][:], 1.0).then_inc(made, 1)
            dve.memset(kept["row_norm"][:], 0.0).then_inc(made, 1)
            dve.wait_ge(loaded, 16)
            dve.tensor_copy(kept["ident16"][:], kept["ident"][:]).then_inc(made, 1)
            dve.wait_ge(made, 3)


SCALE, KEY_SCALE_INV2, NEG_INV2, OUT_SCALE = 0, 1, 2, 3


def load_weights(sp, w_stack, layer, w_raw, w_loaded):
    sp.dma_start(w_raw[:], w_stack[layer].rearrange("(c p) n -> p c n", p=P)).then_inc(w_loaded, 16)


def project(nc, sem, layer, x_in, w_stack, w_raw, w_loaded, kept, values, keys_t, T, DC, D):
    ident, ident16, ones, scales = kept["ident"], kept["ident16"], kept["ones"], kept["scales"]
    row_norm = kept["row_norm"]
    W2 = w_stack.shape[2]
    PAIRS = T // 2

    def named(name):
        return sem(f"{name}_p{layer}")

    w_split, squared = named("w_split"), named("squared")
    x_loaded = [named(f"x_loaded{b}") for b in (0, 1)]
    norms_loaded = [named(f"norms_loaded{r}") for r in range(4)]
    norms_done, norm_ready, ones_made = named("norms_done"), named("norm_ready"), named("ones_made")
    columns_done, all_norm, bound_ready, root_ready, scale_ready = (
        named(n) for n in ("columns_done", "all_norm", "bound_ready", "root_ready", "scale_ready"))
    x_turned, x_hi, x_lo = named("x_turned"), named("x_hi"), named("x_lo")
    values_done, keys_done, values_hi, keys_hi = (
        named(n) for n in ("values_done", "keys_done", "values_hi", "keys_hi"))
    values_lo, keys_lo, keys_turned, keys_stored, own = (
        named(n) for n in ("values_lo", "keys_lo", "keys_turned", "keys_stored", "dve_chain"))

    with ExitStack() as s:
        def sb(name, shape, dt):
            return s.enter_context(nc.sbuf_tensor(f"{name}_p{layer}", shape, dt))

        def ps(name, shape, dt):
            return s.enter_context(nc.psum_tensor(f"{name}_p{layer}", shape, dt))

        w_sq = sb("w_sq", [P, DC, W2], F32R)
        ones_r = sb("ones_r", [P, P], F32R)
        w = sb("w", [P, 2, DC, W2], F32R)
        rows2 = sb("rows2", [P, 4, 2 * D], F32)
        norms = sb("norms", [P, PAIRS], F32)
        small = sb("small", [P, 8], F32)
        exponent = sb("exponent", [P, 1], U32)
        x_rows = sb("x_rows", [P, 2, D], F32)
        x_t = sb("x_t", [P, 2, 2, D], F32R)
        keys = sb("keys", [P, 2, 2, D], F16)
        turned_x = ps("turned_x", [P, 2, BANK], F32)
        p_values = ps("p_values", [P, 2, BANK], F32)
        p_keys = ps("p_keys", [P, 2, BANK], F32)
        p_turned_k = ps("p_turned_k", [P, 2, BANK], F32)
        column_norms = p_turned_k
        turned_k = p_turned_k[:].bitcast(F16).rearrange("p b (h c q) -> p b h c q", h=2, c=DC)

        with nc.Block() as block:
            @block.sync
            def _(sp):
                def load_x(t, b):
                    if from_tile(t, 2):
                        sp.wait_ge(x_turned, t - 1)
                    sp.dma_start(x_rows[:, b], x_in[bass.ds(t * P, P), :]).then_inc(x_loaded[b], 16)

                if layer == 0:
                    load_weights(sp, w_stack, 0, w_raw, w_loaded)
                load_x(0, 0)
                load_x(1, 1)
                if layer == 0:
                    pairs = x_in.rearrange("(j p two) d -> j p (two d)", p=P, two=2)
                    for j in range(PAIRS):
                        if j >= 4:
                            sp.wait_ge(norms_done, j - 3)
                        sp.dma_start(rows2[:, j % 4], pairs[j]).then_inc(norms_loaded[j % 4], 16)
                for t, b in row_tiles(sp, T):
                    if from_tile(t, 2):
                        load_x(t, b)

            @block.gpsimd
            def _(pool):
                pool.wait_ge(norm_ready, 1)
                pool.partition_all_reduce(small[:, 1:2], row_norm[:], P, REDUCE_MAX).then_inc(all_norm, 1)

            @block.scalar
            def _(act):
                def halve_x(t, b):
                    act.wait_ge(x_turned, t + 1)
                    if from_tile(t, 2):
                        act.wait_ge(keys_done, t - 1)
                    act.activation(x_t[:, b, HI], turned_x[:, b], ACT.Copy).then_inc(x_hi, 1)

                act.wait_ge(w_loaded, 16 * (layer + 1))
                act.activation(w_sq[:], w_raw[:], ACT.Square).then_inc(squared, 1)
                halve_x(0, 0)
                halve_x(1, 1)
                if layer == 0:
                    for j in range(PAIRS):
                        act.wait_ge(norms_loaded[j % 4], 16 * (j // 4 + 1))
                        act.activation(rows2[:, j % 4], rows2[:, j % 4], ACT.Square,
                                       accum_out=norms[:, j:j + 1]).then_inc(norms_done, 1)

                act.wait_ge(bound_ready, 1)
                act.activation(small[:, 3:4], small[:, 2:3], ACT.Sqrt).then_inc(root_ready, 1)
                for t, b in row_tiles(act, T):
                    if before_end(t, 1, T) and from_tile(t, 1):
                        halve_x(t + 1, 1 - b)
                    act.wait_ge(values_done, t + 1)
                    act.wait_ge(scale_ready, 1)
                    act.activation(values[:, HI, bass.ds(t, 1), :], p_values[:, b:b + 1], ACT.Copy,
                                   scale=scales[:, SCALE:SCALE + 1]).then_inc(values_hi, 1)
                    act.wait_ge(keys_done, t + 1)
                    if from_tile(t, 2):
                        act.wait_ge(keys_turned, t - 1)
                    act.activation(keys[:, b, HI], p_keys[:, b], ACT.Copy,
                                   scale=scales[:, SCALE:SCALE + 1]).then_inc(keys_hi, 1)

            @block.vector
            def _(dve):
                chain = Chain(dve, own)

                def halve_x(t, b):
                    dve.wait_ge(x_hi, t + 1)
                    dve.tensor_tensor(x_t[:, b, LO], turned_x[:, b], x_t[:, b, HI].bitcast(F32),
                                      ALU.subtract).then_inc(x_lo, 1)

                dve.tensor_copy(ones_r[:], ones[:]).then_inc(ones_made, 1)
                dve.wait_ge(w_loaded, 16 * (layer + 1))
                for c in range(DC):
                    dve.tensor_copy(w[:, HI, c], w_raw[:, c]).then_inc(w_split, 1)
                    dve.wait_ge(w_split, 2 * c + 1)
                    dve.tensor_tensor(w[:, LO, c], w_raw[:, c], w[:, HI, c].bitcast(F32),
                                      ALU.subtract).then_inc(w_split, 1)
                halve_x(0, 0)
                halve_x(1, 1)
                if layer == 0:
                    dve.wait_ge(norms_done, PAIRS)
                    chain.link(dve.reduce_max(row_norm[:], norms[:], AX_X))
                dve.tensor_copy(small[:, 4:5], row_norm[:]).then_inc(norm_ready, 1)
                dve.wait_ge(columns_done, 1)
                chain.link(dve.reduce_max(small[:, 0:1], column_norms[:].rearrange("p a b -> p (a b)"), AX_X))
                dve.wait_ge(all_norm, 1)
                chain.link(dve.tensor_tensor(small[:, 5:6], small[:, 0:1], small[:, 1:2], ALU.mult))
                dve.tensor_scalar(small[:, 2:3], small[:, 5:6], LEAST_BOUND, None, ALU.max).then_inc(bound_ready, 1)
                chain.link(dve.memset(exponent[:], EXPONENT_BITS))
                dve.wait_ge(root_ready, 1)
                chain.link(dve.reciprocal(small[:, 6:7], small[:, 3:4]))
                chain.link(dve.tensor_scalar(small[:, 7:8], small[:, 6:7], TOP, None, ALU.mult))
                chain.link(dve.tensor_tensor(scales[:, SCALE:SCALE + 1].bitcast(U32),
                                             small[:, 7:8].bitcast(U32), exponent[:], ALU.bitwise_and))
                chain.link(dve.reciprocal(small[:, 6:7], scales[:, SCALE:SCALE + 1]))
                chain.link(dve.tensor_tensor(scales[:, KEY_SCALE_INV2:KEY_SCALE_INV2 + 1],
                                             small[:, 6:7], small[:, 6:7], ALU.mult))
                chain.link(dve.tensor_scalar(scales[:, NEG_INV2:NEG_INV2 + 1],
                                             scales[:, KEY_SCALE_INV2:KEY_SCALE_INV2 + 1], -1.0, None, ALU.mult))
                dve.tensor_scalar(scales[:, OUT_SCALE:OUT_SCALE + 1], small[:, 6:7],
                                  1.0 / PROB_SCALE, None, ALU.mult).then_inc(scale_ready, 1)
                scale = scales[:, SCALE:SCALE + 1]

                def store_keys(t, b):
                    dve.wait_ge(keys_turned, t + 1)
                    dve.tensor_scalar(keys_t[:, :, :, bass.ds(t * P, P)], turned_k[:, b], 1.0, None,
                                      ALU.mult).then_inc(keys_stored, 1)

                for t, b in row_tiles(dve, T):
                    if before_end(t, 1, T) and from_tile(t, 1):
                        halve_x(t + 1, 1 - b)
                    if from_tile(t, 1):
                        store_keys(t - 1, 1 - b)
                    dve.wait_ge(values_hi, t + 1)
                    dve.scalar_tensor_tensor(out=values[:, LO, bass.ds(t, 1), :], in0=p_values[:, b:b + 1],
                                             scalar=scale, in1=values[:, HI, bass.ds(t, 1), :],
                                             op0=ALU.mult, op1=ALU.subtract).then_inc(values_lo, 1)
                    dve.wait_ge(keys_hi, t + 1)
                    dve.scalar_tensor_tensor(out=keys[:, b, LO], in0=p_keys[:, b], scalar=scale,
                                             in1=keys[:, b, HI], op0=ALU.mult,
                                             op1=ALU.subtract).then_inc(keys_lo, 1)
                store_keys(T - 1, (T - 1) % 2)

            @block.tensor
            def _(pe):
                def turn_x(t, b):
                    pe.wait_ge(x_loaded[b], landed(t, b))
                    if from_tile(t, 2):
                        pe.wait_ge(x_lo, t - 1)
                    for c in range(DC):
                        last = pe.transpose(turned_x[:, b, c * P:(c + 1) * P],
                                            x_rows[:, b, c * P:(c + 1) * P], ident[:])
                    last.then_inc(x_turned, 1)

                def product(bank, t, b, columns):
                    parts = [(HI, HI), (HI, LO), (LO, HI)]
                    for c in range(DC):
                        if fixed(t) and t == 0:
                            pe.wait_ge(w_split, 2 * (c + 1))
                        for n, (xh, wh) in enumerate(parts):
                            last = pe.matmul(bank, x_t[:, b, xh, c * P:(c + 1) * P], w[:, wh, c, columns],
                                             start=(c == 0 and n == 0), stop=(c == DC - 1 and n == 2))
                    return last

                def turn_keys(t, b):
                    pe.wait_ge(keys_lo, t + 1)
                    if from_tile(t, 2):
                        pe.wait_ge(keys_stored, t - 1)
                    for half in (HI, LO):
                        for c in range(DC):
                            last = pe.transpose(turned_k[:, b, half, c, :],
                                                keys[:, b, half, c * P:(c + 1) * P], ident16[:])
                    last.then_inc(keys_turned, 1)

                turn_x(0, 0)
                turn_x(1, 1)
                pe.wait_ge(squared, 1)
                pe.wait_ge(ones_made, 1)
                for half in range(W2 // BANK):
                    for c in range(DC):
                        last = pe.matmul(column_norms[:, half], ones_r[:],
                                         w_sq[:, c, half * BANK:(half + 1) * BANK],
                                         start=(c == 0), stop=(c == DC - 1))
                last.then_inc(columns_done, 1)
                for t, b in row_tiles(pe, T):
                    if before_end(t, 1, T) and from_tile(t, 1):
                        turn_x(t + 1, 1 - b)
                    pe.wait_ge(x_lo, t + 1)
                    if from_tile(t, 2):
                        pe.wait_ge(values_lo, t - 1)
                    product(p_values[:, b], t, b, slice(0, D)).then_inc(values_done, 1)
                    if from_tile(t, 1):
                        turn_keys(t - 1, 1 - b)
                    if from_tile(t, 2):
                        pe.wait_ge(keys_lo, t - 1)
                    product(p_keys[:, b], t, b, slice(D, 2 * D)).then_inc(keys_done, 1)
                turn_keys(T - 1, (T - 1) % 2)


def attend(nc, sem, layer, x_in, x_first, adj, rows_out, kept, values, keys_t,
           w_stack, w_raw, w_loaded, adj_t, adj_t16, adj_cast, N, NP, T, DC, D, last_layer):
    ident, ident16, ones, scales = kept["ident"], kept["ident16"], kept["ones"], kept["scales"]
    row_norm, var_eps = kept["row_norm"], kept["var_eps"]
    first_layer = layer == 0
    KC = ceil_div(NP, BANK)
    widths = [min(BANK, NP - k * BANK) for k in range(KC)]
    valid = [min(BANK, N - k * BANK) for k in range(KC)]
    PART = NP // PARTS
    GROUP = BANK // P
    G = ceil_div(T, GROUP)
    members = [range(g * GROUP, min(T, (g + 1) * GROUP)) for g in range(G)]
    SLOTS = 4
    LINKS = 9 if last_layer else 6

    def named(name):
        return sem(f"{name}_a{layer}")

    adj_loaded, x_loaded, stored = (
        [named(f"{n}{b}") for b in (0, 1)] for n in ("adj_loaded", "x_loaded", "stored"))
    q_staged, q_turned, q_ready = (named(n) for n in ("q_staged", "q_turned", "q_ready"))
    scores_done, scores_read, shift_ready = (named(n) for n in ("scores_done", "scores_read", "shift_ready"))
    exp_done, masked, pad_zeroed = (named(n) for n in ("exp_done", "masked", "pad_zeroed"))
    probs_turned, probs_hi, probs_split, mixed = (
        named(n) for n in ("probs_turned", "probs_hi", "probs_split", "mixed"))
    adj_anded, adj_checked, adj_low = named("adj_anded"), named("adj_checked"), kept["adj_low"]
    rows_done, own, peak_own = (named(n) for n in ("rows_done", "dve_chain", "peak_chain"))

    with ExitStack() as s:
        def sb(name, shape, dt):
            return s.enter_context(nc.sbuf_tensor(f"{name}_a{layer}", shape, dt))

        def ps(name, shape, dt):
            return s.enter_context(nc.psum_tensor(f"{name}_a{layer}", shape, dt))

        row = sb("row", [P, 2, NP], F32)
        adj_row = sb("adj_row", [P, 2, NP], F32)
        probs = sb("probs", [P, SLOTS, 2, GROUP * P], F16)
        q_rows = sb("q_rows", [P, 2, D], F16)
        q_t = sb("q_t", [P, 2, 2, DC, P], F16)
        peaks = sb("peaks", [P, 2, KC + 1], F32)
        shift = sb("shift", [P, 2], F32)
        sums = sb("sums", [P, 2, PARTS], F32)
        small = sb("small", [P, 16], F32)
        stats = sb("stats", [P, 8], F32)
        waited = sb("waited", [P, 1], F32)
        x_rows = sb("x_rows", [P, 2, D], F32)
        x0_rows = sb("x0_rows", [P, 2, D], F32) if last_layer else None
        work = sb("work", [P, 2, D], F32)
        y_rows = sb("y_rows", [P, 2, D], F32)
        low_words = sb("low_words", [P, PART], U32) if first_layer else None
        p_scores = ps("p_scores", [P, 2, BANK], F32)
        p_probs = ps("p_probs", [P, 2, BANK], F32)
        p_out = ps("p_out", [P, 2, BANK], F32)
        p_q = ps("p_q", [P, 2, DC, P], F16)
        X_LOADS = 2 if last_layer else 1

        with nc.Block() as block:
            @block.sync
            def _(sp):
                def store(t, b):
                    sp.dma_start(rows_out[bass.ds(t * P, P), :], y_rows[:, b]).then_inc(stored[b], 16)

                for t, b in row_tiles(sp, T):
                    if from_tile(t, 2):
                        sp.wait_ge(masked, PARTS * (t - 1))
                        if first_layer:
                            sp.wait_ge(adj_checked, PARTS * (t - 1))
                    if fixed(t) and t == 1 and not last_layer:
                        load_weights(sp, w_stack, layer + 1, w_raw, w_loaded)
                    sp.dma_start(adj_row[:, b], adj[bass.ds(t * P, P), :]).then_inc(adj_loaded[b], 16)
                    if from_tile(t, 2):
                        sp.wait_ge(rows_done, t - 1)
                        store(t - 2, b)
                    sp.dma_start(x_rows[:, b], x_in[bass.ds(t * P, P), :]).then_inc(x_loaded[b], 16)
                    if last_layer:
                        sp.dma_start(x0_rows[:, b], x_first[bass.ds(t * P, P), :]).then_inc(x_loaded[b], 16)
                for t in (T - 2, T - 1):
                    sp.wait_ge(rows_done, t + 1)
                    store(t, t % 2)
                for b in (0, 1):
                    sp.wait_ge(stored[b], 16 * (T // 2))

            @block.tensor
            def _(pe):
                def turn_q(t):
                    pe.wait_ge(q_staged, t + 1)
                    if from_tile(t, 1):
                        pe.wait_ge(q_ready, t)
                    for half in (HI, LO):
                        for c in range(DC):
                            last = pe.transpose(p_q[:, half, c, :], q_rows[:, half, c * P:(c + 1) * P], ident16[:])
                    last.then_inc(q_turned, 1)

                def scores(t, b, chunks):
                    pe.wait_ge(q_ready, t + 1)
                    for k in chunks:
                        bank = (b * KC + k) % 2
                        if from_tile(t, 1) or k >= 2:
                            pe.wait_ge(scores_read, t * KC + k - 1)
                        n = 0
                        for c in range(DC):
                            for qh, kh in ((HI, HI), (HI, LO), (LO, HI)):
                                last = pe.matmul(p_scores[:, bank, 0:widths[k]], q_t[:, b, qh, c, :],
                                                 keys_t[:, kh, c, k * BANK:k * BANK + widths[k]],
                                                 start=(n == 0), stop=(n == 3 * DC - 1))
                                n += 1
                        last.then_inc(scores_done, 1)

                def turn_probs(t, b, g):
                    if from_tile(t, 1) or g >= 2:
                        pe.wait_ge(probs_split, t * G + g - 1)
                    for j, k in enumerate(members[g]):
                        last = pe.transpose(p_probs[:, (b * G + g) % 2, j * P:(j + 1) * P],
                                            row[:, b, k * P:(k + 1) * P], ident[:])
                    last.then_inc(probs_turned, 1)

                def mix(t, b, g):
                    pe.wait_ge(probs_split, t * G + g + 1)
                    for j, k in enumerate(members[g]):
                        for n, (ph, vh) in enumerate(((HI, HI), (HI, LO), (LO, HI))):
                            last = pe.matmul(p_out[:, b], probs[:, g % SLOTS, ph, j * P:(j + 1) * P], values[:, vh, k, :],
                                             start=(k == 0 and n == 0), stop=(k == T - 1 and n == 2))
                    last.then_inc(mixed, 1)

                turn_q(0)
                turn_q(1)
                scores(0, 0, range(KC))
                for t, b in row_tiles(pe, T):
                    if before_end(t, 1, T):
                        scores(t + 1, 1 - b, range(KC - 1))
                    pe.wait_ge(masked, PARTS * (t + 1))
                    turn_probs(t, b, 0)
                    turn_probs(t, b, 1)
                    if before_end(t, 1, T):
                        scores(t + 1, 1 - b, range(KC - 1, KC))
                    if before_end(t, 2, T):
                        turn_q(t + 2)
                    if from_tile(t, 2):
                        pe.wait_ge(rows_done, t - 1)
                    for g in range(G):
                        mix(t, b, g)
                        if g + 2 < G:
                            turn_probs(t, b, g + 2)

            @block.scalar
            def _(act):
                def exp_part(t, b, part):
                    if part == 0:
                        if from_tile(t, 2):
                            act.wait_ge(rows_done, t - 1)
                        act.wait_ge(shift_ready, t + 1)
                    piece = row[:, b, part * PART:min(N, (part + 1) * PART)]
                    act.activation(piece, piece, ACT.Exp, bias=shift[:, b:b + 1],
                                   scale=scales[:, KEY_SCALE_INV2:KEY_SCALE_INV2 + 1],
                                   accum_out=sums[:, b, part:part + 1]).then_inc(exp_done, 1)

                for part in range(PARTS):
                    exp_part(0, 0, part)
                for t, b in row_tiles(act, T):
                    for g in range(G):
                        act.wait_ge(probs_turned, t * G + g + 1)
                        used = len(members[g]) * P
                        act.activation(probs[:, g % SLOTS, HI, 0:used], p_probs[:, (b * G + g) % 2, 0:used],
                                       ACT.Copy, scale=PROB_SCALE).then_inc(probs_hi, 1)
                        if 1 <= g <= PARTS and before_end(t, 1, T):
                            exp_part(t + 1, 1 - b, g - 1)

            @block.gpsimd
            def _(pool):
                for t, b in row_tiles(pool, T):
                    pool.wait_ge(adj_loaded[b], landed(t, b))
                    pool.wait_ge(pad_zeroed, 2)
                    for part in range(PARTS):
                        pool.wait_ge(exp_done, t * PARTS + part + 1)
                        piece = slice(part * PART, (part + 1) * PART)
                        pool.tensor_tensor(row[:, b, piece], row[:, b, piece], adj_row[:, b, piece],
                                           ALU.mult).then_inc(masked, 1)
                    if last_layer:
                        pool.dma_start(adj_t16[bass.ds(t * P, P), :],
                                       adj_t[bass.ds(t * P, P), :]).then_inc(adj_cast, 16)
                if last_layer:
                    pool.wait_ge(adj_cast, 16 * T)

            @block.vector
            def _(dve):
                peak_chain, chain = Chain(dve, peak_own, 1), Chain(dve, own, LINKS)

                def stage_q(t):
                    if from_tile(t, 1):
                        dve.wait_ge(q_turned, t)
                    dve.tensor_scalar(q_rows[:].rearrange("p (h o) d -> p h o d", o=1),
                                      values[:, :, bass.ds(t, 1), :], 1.0, None, ALU.mult).then_inc(q_staged, 1)

                def copy_q(t, b):
                    dve.wait_ge(q_turned, t + 1)
                    if from_tile(t, 2):
                        dve.wait_ge(scores_done, (t - 1) * KC)
                    dve.tensor_copy(q_t[:, b], p_q[:]).then_inc(q_ready, 1)

                def read_scores(t, b, k):
                    if k == 0 and from_tile(t, 2):
                        dve.wait_ge(probs_turned, (t - 1) * G)
                    dve.wait_ge(scores_done, t * KC + k + 1)
                    dve.wait_ge(pad_zeroed, 2)
                    w = valid[k]
                    dve.tensor_scalar(row[:, b, k * BANK:k * BANK + w], p_scores[:, (b * KC + k) % 2, 0:w],
                                      1.0, LOWEST, ALU.mult, ALU.max,
                                      accum_out=peaks[:, b, k:k + 1]).then_inc(scores_read, 1)

                def make_shift(t, b):
                    peak_chain.tile(t)
                    dve.wait_ge(scores_read, (t + 1) * KC)
                    peak_chain.link(dve.reduce_max(peaks[:, b, KC:KC + 1], peaks[:, b, 0:KC], AX_X))
                    dve.tensor_tensor(shift[:, b:b + 1], peaks[:, b, KC:KC + 1],
                                      scales[:, NEG_INV2:NEG_INV2 + 1], ALU.mult).then_inc(shift_ready, 1)

                def split_probs(t, b, g):
                    dve.wait_ge(probs_hi, t * G + g + 1)
                    used = len(members[g]) * P
                    dve.scalar_tensor_tensor(out=probs[:, g % SLOTS, LO, 0:used], in0=p_probs[:, (b * G + g) % 2, 0:used],
                                             scalar=PROB_SCALE, in1=probs[:, g % SLOTS, HI, 0:used],
                                             op0=ALU.mult, op1=ALU.subtract).then_inc(probs_split, 1)

                def finish(t, b):
                    chain.tile(t)
                    r = small[:, 8 * b:8 * b + 8]
                    dve.wait_ge(mixed, (t + 1) * G)
                    chain.link(dve.reduce_sum(r[:, 0:1], sums[:, b], AX_X))
                    chain.link(dve.reciprocal(r[:, 1:2], r[:, 0:1]))
                    chain.link(dve.tensor_tensor(r[:, 2:3], r[:, 1:2], scales[:, OUT_SCALE:OUT_SCALE + 1], ALU.mult))
                    dve.wait_ge(x_loaded[b], landed(t, b, X_LOADS))
                    chain.link(dve.scalar_tensor_tensor(out=work[:, b], in0=p_out[:, b], scalar=r[:, 2:3],
                                                        in1=x_rows[:, b], op0=ALU.mult, op1=ALU.add))
                    if from_tile(t, 2):
                        dve.wait_ge(stored[b], landed(t - 2, b))
                    chain.link(dve.scalar_tensor_tensor(out=y_rows[:, b], in0=work[:, b], scalar=SLOPE,
                                                        in1=work[:, b], op0=ALU.mult, op1=ALU.max))
                    if last_layer:
                        chain.link(dve.tensor_tensor(work[:, b], y_rows[:, b], x0_rows[:, b], ALU.add))

                def measure(t, b):
                    r = small[:, 8 * b:8 * b + 8]
                    if not last_layer:
                        chain.link(dve.tensor_tensor_reduce(work[:, b], y_rows[:, b], y_rows[:, b], 1.0, 0.0,
                                                            ALU.mult, ALU.add, r[:, 3:4]))
                        dve.tensor_tensor(row_norm[:], row_norm[:], r[:, 3:4], ALU.max).then_inc(rows_done, 1)
                    else:
                        chain.link(dve.bn_stats(stats[:, 0:6], work[:, b]))
                        dve.memset(waited[:], 0.0)
                        chain.link(dve.bn_aggr(stats[:, 6:8], stats[:, 0:6]))
                        chain.link(dve.tensor_scalar(var_eps[:, bass.ds(t, 1)], stats[:, 7:8], EPS, None, ALU.add))
                        dve.tensor_scalar(y_rows[:, b], work[:, b], stats[:, 6:7], None,
                                          ALU.subtract).then_inc(rows_done, 1)
                    assert chain.done == LINKS

                def check_adj(t, b, part):
                    dve.wait_ge(adj_loaded[b], landed(t, b))
                    if from_tile(t, 1) or part > 0:
                        dve.wait_ge(adj_checked, t * PARTS + part)
                    dve.tensor_scalar(low_words[:], adj_row[:, b, part * PART:(part + 1) * PART].bitcast(U32),
                                      LOW_BITS, None, ALU.bitwise_and).then_inc(adj_anded, 1)
                    dve.wait_ge(adj_anded, t * PARTS + part + 1)
                    dve.wait_ge(pad_zeroed, 2)
                    dve.reduce_max(adj_low[:, bass.ds(t * PARTS + part, 1)], low_words[:],
                                   AX_X).then_inc(adj_checked, 1)

                for b in (0, 1):
                    dve.memset(row[:, b, N:NP], 0.0).then_inc(pad_zeroed, 1)
                stage_q(0)
                copy_q(0, 0)
                stage_q(1)
                copy_q(1, 1)
                for k in range(KC):
                    read_scores(0, 0, k)
                make_shift(0, 0)
                if first_layer:
                    for part in range(PARTS):
                        check_adj(0, 0, part)
                for t, b in row_tiles(dve, T):
                    ahead = before_end(t, 1, T)
                    if ahead:
                        read_scores(t + 1, 1 - b, 0)
                    if from_tile(t, 1):
                        finish(t - 1, 1 - b)
                    if ahead:
                        read_scores(t + 1, 1 - b, 1)
                    if from_tile(t, 1):
                        measure(t - 1, 1 - b)
                    if ahead:
                        for k in range(2, KC - 1):
                            read_scores(t + 1, 1 - b, k)
                    if before_end(t, 2, T):
                        stage_q(t + 2)
                    split_probs(t, b, 0)
                    split_probs(t, b, 1)
                    if ahead:
                        read_scores(t + 1, 1 - b, KC - 1)
                        make_shift(t + 1, 1 - b)
                    if before_end(t, 2, T):
                        copy_q(t + 2, b)
                    for g in range(2, G):
                        split_probs(t, b, g)
                        if first_layer and ahead and g - 2 < PARTS:
                            check_adj(t + 1, 1 - b, g - 2)
                finish(T - 1, (T - 1) % 2)
                measure(T - 1, (T - 1) % 2)


def binary_layer(nc, sem, centred, weight, adj_t, adj_t16, out, kept, T, DC, D):
    ident, ident16, var_eps, adj_low = (kept[n] for n in ("ident", "ident16", "var_eps", "adj_low"))
    names = ("weight_loaded", "weight_turned", "signs_made", "above", "rows_turned", "rows_copied",
             "products_done", "products_kept", "roots", "rstd_made", "low_bits_found", "low_bits_max",
             "low_bits_ready", "adj_hi_made", "adj_lo_made", "sums_done", "var_made", "std_made",
             "rows_done", "dve_chain", "products_wide")
    (weight_loaded, weight_turned, signs_made, above, rows_turned, rows_copied,
     products_done, products_kept, roots, rstd_made, low_bits_found, low_bits_max,
     low_bits_ready, adj_hi_made, adj_lo_made, sums_done, var_made, std_made,
     rows_done, own, products_wide) = (sem(f"{n}_b") for n in names)
    adj_loaded, y_loaded, stored = (
        [sem(f"{n}{b}_b") for b in (0, 1)] for n in ("adj_loaded", "y_loaded", "stored"))
    rows_loaded, adj16_loaded = (
        [sem(f"{n}{r}_b") for r in range(4)] for n in ("rows_loaded", "adj16_loaded"))
    LINKS = 5

    with ExitStack() as s:
        def sb(name, shape, dt):
            return s.enter_context(nc.sbuf_tensor(f"{name}_b", shape, dt))

        def ps(name, shape, dt):
            return s.enter_context(nc.psum_tensor(f"{name}_b", shape, dt))

        products = sb("products", [P, T, D], F16)
        products_r = sb("products_r", [P, T, D], F32R)
        w_rows = sb("w_rows", [P, DC, D], F32)
        positive = sb("positive", [P, DC, D], F16)
        negative = sb("negative", [P, DC, D], F16)
        signs_t = sb("signs_t", [P, DC, D], F16)
        rows = sb("rows", [P, 4, D], F32)
        bits = sb("bits", [P, 4, D], F16)
        bits_t = sb("bits_t", [P, 4, DC * P], F16)
        root = sb("root", [P, T], F32)
        rstd = sb("rstd", [P, T], F32)
        flag = sb("flag", [P, 2], F32)
        has_low = sb("has_low", [P, 1], mybir.dt.int32)
        adj16 = sb("adj16", [P, 4, T * P], BF16)
        adj_raw = sb("adj_raw", [P, 1, T * P], F32)
        adj_hi = sb("adj_hi", [P, 1, T * P], F32R)
        adj_lo = sb("adj_lo", [P, 1, T * P], F32R)
        y_in = sb("y_in", [P, 2, D], F32)
        work = sb("work", [P, 2, D], F32)
        y_rows = sb("y_rows", [P, 2, D], F32)
        stats = sb("stats", [P, 2, 8], F32)
        std = sb("std", [P, 2, 4], F32)
        waited = sb("waited", [P, 1], F32)
        p_w = ps("p_w", [P, DC, BANK], F32)
        p_bits = ps("p_bits", [P, 2, 2 * BANK], F16)
        p_out = ps("p_out", [P, 2, BANK], F32)

        def by_low_bits(engine, body):
            engine.wait_ge(low_bits_ready, 1)
            low = engine.value_load(has_low[0:1, 0:1], min_val=0, max_val=LOW_BITS)
            with engine.If(low > 0):
                body(True)
            with engine.Else():
                body(False)

        with nc.Block() as block:
            @block.sync
            def _(sp):
                def load_rows(t, r):
                    if from_tile(t, 4):
                        sp.wait_ge(above, t - 3)
                    sp.dma_start(rows[:, r], centred[bass.ds(t * P, P), :]).then_inc(rows_loaded[r], 16)

                def load_adj16(t, r):
                    sp.dma_start(adj16[:, r], adj_t16[bass.ds(t * P, P), :]).then_inc(adj16_loaded[r], 16)

                def tiles_of(split):
                    if split:
                        for t, b in row_tiles(sp, T):
                            if from_tile(t, 1):
                                sp.wait_ge(adj_lo_made, t)
                            sp.dma_start(adj_raw[:, 0], adj_t[bass.ds(t * P, P), :]).then_inc(adj_loaded[0], 16)
                    else:
                        for t, r in quad_tiles(sp, T):
                            if from_tile(t, 4):
                                sp.wait_ge(sums_done, t - 3)
                                load_adj16(t, r)

                sp.dma_start(w_rows[:], weight.rearrange("(r p) n -> p r n", p=P)).then_inc(weight_loaded, 16)
                for t, r in quad_tiles(sp, T):
                    load_rows(t, r)
                for t in range(4):
                    load_adj16(t, t)
                by_low_bits(sp, tiles_of)

            @block.gpsimd
            def _(pool):
                pool.wait_ge(low_bits_found, 1)
                pool.partition_all_reduce(flag[:, 1:2], flag[:, 0:1], P, REDUCE_MAX).then_inc(low_bits_max, 1)

            @block.tensor
            def _(pe):
                pe.wait_ge(weight_loaded, 16)
                for c in range(DC):
                    for r in range(DC):
                        last = pe.transpose(p_w[:, c, r * P:(r + 1) * P], w_rows[:, r, c * P:(c + 1) * P], ident[:])
                last.then_inc(weight_turned, 1)

                def turn(t, r):
                    pe.wait_ge(above, t + 1)
                    if from_tile(t, 2):
                        pe.wait_ge(rows_copied, t - 1)
                    for c in range(DC):
                        last = pe.transpose(p_bits[:, r % 2, c * P:(c + 1) * P], bits[:, r, c * P:(c + 1) * P],
                                            ident16[:])
                    last.then_inc(rows_turned, 1)

                turn(0, 0)
                turn(1, 1)
                pe.wait_ge(signs_made, 3)
                for t, r in quad_tiles(pe, T):
                    pe.wait_ge(rows_copied, t + 1)
                    if from_tile(t, 2):
                        pe.wait_ge(products_kept, t - 1)
                    for c in range(DC):
                        last = pe.matmul(p_out[:, r % 2], bits_t[:, r, c * P:(c + 1) * P], signs_t[:, c],
                                         start=(c == 0), stop=(c == DC - 1))
                    last.then_inc(products_done, 1)
                    if before_end(t, 2, T):
                        turn(t + 2, (r + 2) % 4)
                pe.wait_ge(products_kept, T)

                def tiles_of(split):
                    if split:
                        for t, b in row_tiles(pe, T):
                            pe.wait_ge(adj_lo_made, t + 1)
                            pe.wait_ge(products_wide, 1)
                            if from_tile(t, 2):
                                pe.wait_ge(rows_done, t - 1)
                            for k in range(T):
                                for half in (adj_hi, adj_lo):
                                    last = pe.matmul(p_out[:, b], half[:, 0, k * P:(k + 1) * P], products_r[:, k, :],
                                                     start=(k == 0 and half is adj_hi),
                                                     stop=(k == T - 1 and half is adj_lo))
                            last.then_inc(sums_done, 1)
                    else:
                        for t, r in quad_tiles(pe, T):
                            pe.wait_ge(adj16_loaded[r], landed(t, r, ring=4))
                            if from_tile(t, 2):
                                pe.wait_ge(rows_done, t - 1)
                            for k in range(T):
                                last = pe.matmul(p_out[:, r % 2], adj16[:, r, k * P:(k + 1) * P], products[:, k, :],
                                                 start=(k == 0), stop=(k == T - 1))
                            last.then_inc(sums_done, 1)

                by_low_bits(pe, tiles_of)

            @block.scalar
            def _(act):
                act.activation(root[:], var_eps[:], ACT.Sqrt).then_inc(roots, 1)
                for t, r in quad_tiles(act, T):
                    act.wait_ge(rows_turned, t + 1)
                    if from_tile(t, 4):
                        act.wait_ge(products_done, t - 3)
                    act.activation(bits_t[:, r], p_bits[:, r % 2, 0:DC * P], ACT.Copy).then_inc(rows_copied, 1)

                def load_y(t, b):
                    act.dma_start(y_in[:, b], centred[bass.ds(t * P, P), :]).then_inc(y_loaded[b], 16)

                def copy_hi(t):
                    act.wait_ge(adj_loaded[0], 16 * (t + 1))
                    if from_tile(t, 1):
                        act.wait_ge(sums_done, t)
                    act.activation(adj_hi[:, 0], adj_raw[:, 0], ACT.Copy).then_inc(adj_hi_made, 1)

                load_y(0, 0)
                load_y(1, 1)

                def tiles_of(split):
                    for t, b in row_tiles(act, T):
                        if split:
                            copy_hi(t)
                        act.wait_ge(var_made, t + 1)
                        act.activation(std[:, b, 1:2], std[:, b, 0:1], ACT.Sqrt).then_inc(std_made, 1)
                        act.wait_ge(rows_done, t + 1)
                        act.dma_start(out[bass.ds(t * P, P), :], y_rows[:, b]).then_inc(stored[b], 16)
                        if before_end(t, 2, T):
                            load_y(t + 2, b)

                by_low_bits(act, tiles_of)
                for b in (0, 1):
                    act.wait_ge(stored[b], 16 * (T // 2))

            @block.vector
            def _(dve):
                def compare(t, r):
                    dve.wait_ge(rows_loaded[r], landed(t, r, ring=4))
                    if from_tile(t, 4):
                        dve.wait_ge(rows_turned, t - 3)
                    dve.tensor_scalar(bits[:, r], rows[:, r], 0.0, None, ALU.is_gt).then_inc(above, 1)

                dve.wait_ge(weight_turned, 1)
                dve.tensor_scalar(positive[:], p_w[:], 0.0, None, ALU.is_gt).then_inc(signs_made, 1)
                dve.tensor_scalar(negative[:], p_w[:], 0.0, None, ALU.is_lt).then_inc(signs_made, 1)
                for t in range(2):
                    compare(t, t)
                dve.wait_ge(signs_made, 2)
                dve.tensor_tensor(signs_t[:], positive[:], negative[:], ALU.subtract).then_inc(signs_made, 1)
                dve.reduce_max(flag[:, 0:1], adj_low[:], AX_X).then_inc(low_bits_found, 1)
                dve.wait_ge(roots, 1)
                dve.reciprocal(rstd[:], root[:]).then_inc(rstd_made, 1)
                dve.wait_ge(low_bits_max, 1)
                dve.tensor_copy(has_low[:], flag[:, 1:2]).then_inc(low_bits_ready, 1)
                for t, r in quad_tiles(dve, T):
                    if before_end(t, 2, T):
                        compare(t + 2, (r + 2) % 4)
                    dve.wait_ge(products_done, t + 1)
                    dve.tensor_scalar(products[:, bass.ds(t, 1), :], p_out[:, r % 2:r % 2 + 1], 1.0, None,
                                      ALU.mult).then_inc(products_kept, 1)
                dve.wait_ge(rstd_made, 1)

                def make_lo(t):
                    dve.wait_ge(adj_hi_made, t + 1)
                    dve.tensor_tensor(adj_lo[:, 0], adj_raw[:, 0], adj_hi[:, 0].bitcast(F32),
                                      ALU.subtract).then_inc(adj_lo_made, 1)

                def tiles_of(split):
                    chain = Chain(dve, own, LINKS)
                    if split:
                        dve.wait_ge(products_kept, T)
                        dve.tensor_copy(products_r[:], products[:]).then_inc(products_wide, 1)
                    for t, b in row_tiles(dve, T):
                        if split:
                            make_lo(t)
                        chain.tile(t)
                        dve.wait_ge(y_loaded[b], landed(t, b))
                        chain.link(dve.tensor_scalar(work[:, b], y_in[:, b], rstd[:, bass.ds(t, 1)], None, ALU.mult))
                        dve.wait_ge(sums_done, t + 1)
                        chain.link(dve.scalar_tensor_tensor(out=work[:, b], in0=p_out[:, b], scalar=0.0,
                                                            in1=work[:, b], op0=ALU.max, op1=ALU.add))
                        chain.link(dve.bn_stats(stats[:, b, 0:6], work[:, b]))
                        dve.memset(waited[:], 0.0)
                        chain.link(dve.bn_aggr(stats[:, b, 6:8], stats[:, b, 0:6]))
                        dve.tensor_scalar(std[:, b, 0:1], stats[:, b, 7:8], EPS, None, ALU.add).then_inc(var_made, 1)
                        dve.wait_ge(std_made, t + 1)
                        chain.link(dve.reciprocal(std[:, b, 2:3], std[:, b, 1:2]))
                        if from_tile(t, 2):
                            dve.wait_ge(stored[b], landed(t - 2, b))
                        dve.tensor_scalar(y_rows[:, b], work[:, b], stats[:, b, 6:7], std[:, b, 2:3],
                                          ALU.subtract, ALU.mult).then_inc(rows_done, 1)
                        assert chain.done == LINKS

                by_low_bits(dve, tiles_of)


def kernel(x, adj, L0_gnn_W_stack, L1_gnn_weight):
    import numpy as np
    import concourse.bacc as bacc
    from concourse.bass_utils import run_bass_kernel_spmd

    x, adj = np.asarray(x), np.asarray(adj)
    n, d = x.shape
    padded = ceil_div(n, P) * P
    tiles = padded // P
    x_rows = np.zeros((padded, d), x.dtype)
    x_rows[:n] = x
    adj_rows = np.zeros((padded, padded), adj.dtype)
    adj_rows[:n, :n] = adj
    adj_blocks = np.ascontiguousarray(adj_rows.reshape(tiles, P, tiles, P).transpose(0, 3, 2, 1))
    arrays = {
        "x_rows": x_rows,
        "adj_rows": adj_rows,
        "adj_blocks": adj_blocks.reshape(padded, padded),
        "w_stack": np.ascontiguousarray(L0_gnn_W_stack),
        "weight": np.ascontiguousarray(L1_gnn_weight),
        "identity": np.eye(P, dtype=np.float32),
    }
    nc = bacc.Bacc("TRN2", target_bir_lowering=False, num_devices=1)
    aps = [nc.dram_tensor(name, a.shape, mybir.dt.from_np(a.dtype), kind="ExternalInput").ap()
           for name, a in arrays.items()]
    result = nc.dram_tensor("result", (padded, d), F32, kind="ExternalOutput").ap()
    build(nc, n, *aps, result)
    got = run_bass_kernel_spmd(nc, [arrays], core_ids=[0])
    return got.results[0]["result"][:n]
```
